# Optimizing a Trainium2 kernel written in Bass

```python
import numpy as np
import jax
import jax.numpy as jnp

def _softmax(x, axis=-1):
    return jax.nn.softmax(x, axis=axis)

def _gelu(x):
    return jax.nn.gelu(x, approximate=True)

def _silu(x):
    return jax.nn.silu(x)

def _sigmoid(x):
    return jax.nn.sigmoid(x)

def _layernorm(x, axis=-1, eps=1e-05):
    m = jnp.mean(x, axis=axis, keepdims=True)
    v = jnp.var(x, axis=axis, keepdims=True)
    return (x - m) / jnp.sqrt(v + eps)

def _scatter_add(tgt, idx, src, axis=0):
    return tgt.at[idx].add(src)

def _segment_sum(src, seg, n):
    return jax.ops.segment_sum(src, seg, n)
kernel_name = 'mk_sandwich_d1_jaxref_r4_7a4c79'

def setup_inputs(seed: int=0):
    np.random.seed(seed)
    _w = jnp.asarray

    def _L0_attn_setup():
        import jax, jax.numpy as jnp
        import numpy as np
        B, N, D = (8, 256, 256)
        H = 16
        HD = D // H
        key = jax.random.key(seed)
        ks = jax.random.split(key, 5)
        s = 0.02
        return {'x': jax.random.normal(ks[0], (B, N, D), dtype=jnp.float32), 'w_attn': jax.random.normal(ks[1], (D, 3 * D), dtype=jnp.float32) * s, 'b_attn': jnp.zeros((3 * D,), dtype=jnp.float32), 'w_proj': jax.random.normal(ks[2], (D, D), dtype=jnp.float32) * s, 'b_proj': jnp.zeros((D,), dtype=jnp.float32)}
    _L0_attn_in = _L0_attn_setup()

    def _L0_ffn_setup():
        import jax, jax.numpy as jnp
        import numpy as np
        D_IN, D_HID = (256, 1024)

        def _ternary(key, shape):
            return jax.random.randint(key, shape, -1, 2).astype(jnp.float32)

        def _tlin(x, w, s):
            return jnp.einsum('bsi,oi->bso', x, w) * s
        key = jax.random.key(seed)
        ks = jax.random.split(key, 12)
        inv = lambda fan: 1.0 / np.sqrt(fan).astype(np.float32)
        return {'x': jax.random.normal(ks[0], (4, 512, D_IN), dtype=jnp.float32), 'w1_w': _ternary(ks[1], (D_HID, D_IN)), 'w1_s': jax.random.uniform(ks[2], (D_HID,), dtype=jnp.float32) * inv(D_IN), 'w2_w': _ternary(ks[3], (D_HID, D_IN)), 'w2_s': jax.random.uniform(ks[4], (D_HID,), dtype=jnp.float32) * inv(D_IN), 'h1_w': _ternary(ks[5], (D_HID, D_HID)), 'h1_s': jax.random.uniform(ks[6], (D_HID,), dtype=jnp.float32) * inv(D_HID), 'h2_w': _ternary(ks[7], (D_HID, D_HID)), 'h2_s': jax.random.uniform(ks[8], (D_HID,), dtype=jnp.float32) * inv(D_HID), 'w3_w': _ternary(ks[9], (D_IN, D_HID)), 'w3_s': jax.random.uniform(ks[10], (D_IN,), dtype=jnp.float32) * inv(D_HID)}
    _L0_ffn_in = _L0_ffn_setup()
    _d = {'L0_attn_x': _L0_attn_in['x'], 'L0_attn_w_attn': _L0_attn_in['w_attn'], 'L0_attn_b_attn': _L0_attn_in['b_attn'], 'L0_attn_w_proj': _L0_attn_in['w_proj'], 'L0_attn_b_proj': _L0_attn_in['b_proj'], 'L0_ffn_w1_w': _L0_ffn_in['w1_w'], 'L0_ffn_w1_s': _L0_ffn_in['w1_s'], 'L0_ffn_w2_w': _L0_ffn_in['w2_w'], 'L0_ffn_w2_s': _L0_ffn_in['w2_s'], 'L0_ffn_h1_w': _L0_ffn_in['h1_w'], 'L0_ffn_h1_s': _L0_ffn_in['h1_s'], 'L0_ffn_h2_w': _L0_ffn_in['h2_w'], 'L0_ffn_h2_s': _L0_ffn_in['h2_s'], 'L0_ffn_w3_w': _L0_ffn_in['w3_w'], 'L0_ffn_w3_s': _L0_ffn_in['w3_s']}
    _x0 = _d['L0_attn_x']
    _d['L0_attn_x'] = jax.random.normal(jax.random.fold_in(jax.random.key(seed), 1), (1, 4096, 256), dtype=_x0.dtype)
    del _x0
    return _d

def reference(L0_attn_x, L0_attn_w_attn, L0_attn_b_attn, L0_attn_w_proj, L0_attn_b_proj, L0_ffn_w1_w, L0_ffn_w1_s, L0_ffn_w2_w, L0_ffn_w2_s, L0_ffn_h1_w, L0_ffn_h1_s, L0_ffn_h2_w, L0_ffn_h2_s, L0_ffn_w3_w, L0_ffn_w3_s):

    def _L0_attn_ref(x, w_attn, b_attn, w_proj, b_proj):
        import jax, jax.numpy as jnp
        import numpy as np
        B, N, D = (8, 256, 256)
        H = 16
        HD = D // H
        b, n, d = x.shape
        hd = d // H
        scale = hd ** (-0.5)
        qkv = x @ w_attn + b_attn
        q, k, v = jnp.split(qkv, 3, axis=-1)
        q = q.reshape(b, n, H, hd).transpose(0, 2, 1, 3)
        k = k.reshape(b, n, H, hd).transpose(0, 2, 1, 3)
        v = v.reshape(b, n, H, hd).transpose(0, 2, 1, 3)
        logits = jnp.einsum('bhqd,bhkd->bhqk', q, k) * scale
        causal = jnp.tril(jnp.ones((n, n), dtype=bool))
        logits = jnp.where(causal[None, None, :, :], logits, -jnp.inf)
        weights = jax.nn.softmax(logits, axis=-1)
        out = jnp.einsum('bhqk,bhkd->bhqd', weights, v)
        out = out.transpose(0, 2, 1, 3).reshape(b, n, d)
        return out @ w_proj + b_proj

    def _L0_ffn_ref(x, w1_w, w1_s, w2_w, w2_s, h1_w, h1_s, h2_w, h2_s, w3_w, w3_s):
        import jax, jax.numpy as jnp
        import numpy as np
        D_IN, D_HID = (256, 1024)

        def _ternary(key, shape):
            return jax.random.randint(key, shape, -1, 2).astype(jnp.float32)

        def _tlin(x, w, s):
            return jnp.einsum('bsi,oi->bso', x, w) * s
        h = jax.nn.silu(_tlin(x, w1_w, w1_s)) * _tlin(x, w2_w, w2_s)
        h = jax.nn.gelu(_tlin(h, h1_w, h1_s), approximate=False)
        h = jax.nn.gelu(_tlin(h, h2_w, h2_s), approximate=False)
        return _tlin(h, w3_w, w3_s)
    x = L0_attn_x
    x = x + _layernorm(_L0_attn_ref(_layernorm(x, axis=-1), L0_attn_w_attn, L0_attn_b_attn, L0_attn_w_proj, L0_attn_b_proj), axis=-1)
    x = x + _layernorm(_L0_ffn_ref(_layernorm(x, axis=-1), L0_ffn_w1_w, L0_ffn_w1_s, L0_ffn_w2_w, L0_ffn_w2_s, L0_ffn_h1_w, L0_ffn_h1_s, L0_ffn_h2_w, L0_ffn_h2_s, L0_ffn_w3_w, L0_ffn_w3_s), axis=-1)
    return x

_drawn_inputs = setup_inputs


def setup_inputs(seed=0):
    import zlib

    import numpy as np

    out = dict(_drawn_inputs(seed))
    spreads = {'L0_attn_b_attn': (0.0, 0.1), 'L0_attn_b_proj': (0.0, 0.1)}
    factors = {}
    for name, (base, spread) in spreads.items():
        noise = np.random.default_rng([zlib.crc32(name.encode()), seed]).standard_normal(out[name].shape)
        drawn = base * np.exp(spread * noise) if base else spread * noise
        out[name] = jnp.asarray(drawn.astype(out[name].dtype))
    for name, factor in factors.items():
        out[name] = (out[name] * factor).astype(out[name].dtype)
    return out
```

```python
from contextlib import ExitStack

import concourse.bass as bass
from concourse import mybir

F32 = mybir.dt.float32
BF = mybir.dt.bfloat16
ALU = mybir.AluOpType
ACT = mybir.ActivationFunctionType
AX = mybir.AxisListType

T = 4096
D = 256
H = 16
HD = 16
F = 1024
CW = 512
NC = T // CW
GH = 4
NG = H // GH
SLOTS = 4
NEG = -1.0e30
EPS = 1e-5
KPART = [0, 0, 1, 0, 2, 1]
QPART = [0, 1, 0, 2, 0, 1]
ROWS = 96


class Count:

    def __init__(self, handle):
        self.handle = handle
        self.n = 0


class Program:

    def __init__(self):
        self.queues = {k: [] for k in ("sync", "tensor", "vector", "scalar", "gpsimd")}

    def put(self, engine, make, wait=(), inc=None):
        wait = [w for w in wait if w is not None]
        step = None
        if inc is not None:
            step = 16 if engine == "sync" or isinstance(make, Dma) else 1
            inc.n += step
        self.queues[engine].append((make, wait, inc, step))
        return (inc, inc.n) if inc is not None else None

    def run(self, engine, e):
        reached = {}
        for make, wait, inc, step in self.queues[engine]:
            for sem, value in wait:
                if reached.get(id(sem), 0) < value:
                    e.wait_ge(sem.handle, value)
                    reached[id(sem)] = value
            ins = make(e)
            if inc is not None:
                ins.then_inc(inc.handle, step)


class Dma:
    def __init__(self, dst, src):
        self.dst, self.src = dst, src

    def __call__(self, e):
        return e.dma_start(self.dst, self.src)


def build(nc, x, w_attn, b_attn, b_qk, w_proj, b_proj, w1t, w1_s, w2t, w2_s, h1t, h1_s, h2t, h2_s,
          w3t, w3_s, ident, out):
    scr = nc.dram_tensor("qk_parts", (3, 2 * D, T), BF, kind="Internal").ap()
    mscr = nc.dram_tensor("row_max", (NG * NC, 3, GH * CW), BF, kind="Internal").ap()
    oscr = nc.dram_tensor("attn_out", (D, T), F32, kind="Internal").ap()
    dscr = nc.dram_tensor("attn_den", (H, T), F32, kind="Internal").ap()

    ctx = ExitStack()
    with ctx:
        def sb(name, shape, dt=F32):
            return ctx.enter_context(nc.sbuf_tensor(name, shape, dt))

        def sem(name):
            return Count(ctx.enter_context(nc.semaphore(name)))

        r1 = sb("r1", [128, 16384])
        r2 = sb("r2", [128, 4096 + 4096])
        r4 = sb("r4", [128, 18432])
        V = sb("V", [128, T // 128, H, HD + 1])
        idf = sb("idf", [128, 128])
        idb = sb("idb", [128, 128], BF)
        mask_q = sb("mask_q", [128, 128], BF)
        mask_k = sb("mask_k", [128, 128], BF)
        wa = r2[:, 4096:5632].rearrange("p (k n) -> p k n", k=2)
        ba = sb("ba", [128, 4])
        bv = sb("bv", [128, D])
        stats = sb("stats", [128, 4, 6])
        mv = sb("mv", [128, 4, 2])
        ve = sb("ve", [128, 4])
        rstd = sb("rstd", [128, 4])
        half = sb("half", [128, 4])
        mp = sb("mp", [128, 2, 16, NC])
        mm = sb("mm", [128, 16])
        m1 = sb("m1", [16, 3, 128], BF)
        mr = sb("mr", [16, 128])
        ps = ctx.enter_context(nc.psum_tensor("ps", [128, 8, 512], F32))

        KS = r1[:, :].bitcast(BF).rearrange("p (b h t) -> p b h t", b=2, h=GH)
        QS = r2[:, 0:4096].bitcast(BF).rearrange("p (s h t) -> p s h t", s=SLOTS, h=GH)
        PB = r2[:, 4096:8192].rearrange("p (n h t) -> p n h t", n=4, h=2)

        P = Program()
        put = P.put

        s_ld = sem("s_ld")
        s_id = sem("s_id")
        s_c = sem("s_c")
        t_id = put("sync", Dma(idf[:, :], ident), inc=s_id)
        s_w = sem("s_w")
        put("sync", Dma(wa, w_attn.rearrange("(k p) n -> p k n", p=128)), inc=s_w)
        put("sync", Dma(ba[:, :], b_qk), inc=s_w)
        t_w = put("sync", Dma(bv[:, :], b_attn[2 * D:3 * D].rearrange("(a n) -> a n", a=1)
                              .to_broadcast([128, D])), inc=s_w)
        put("vector", lambda e: e.memset(half[:, :], -0.5), inc=s_c)
        put("vector", lambda e: e.memset(V[:, :, :, HD:HD + 1], 1.0), inc=s_c)
        put("vector", lambda e: e.memset(ps[:, 6:8, :], 0.0), inc=s_c)
        for b in range(2):
            put("vector", lambda e, b=b: e.memset(KS[ROWS:ROWS + 3, b, :, :], 1.0), inc=s_c)
        t_c = put("vector", lambda e: e.tensor_copy(idb[:, :], idf[:, :]), [t_id], s_c)
        s_g = sem("s_g")
        put("gpsimd", lambda e: e.memset(mask_q[:, :], 0.0), inc=s_g)
        t_g = put("gpsimd", lambda e: e.memset(mask_k[:, :], 0.0), inc=s_g)
        put("gpsimd", lambda e: e.affine_select(out=mask_q[:, :], in_=mask_q[:, :],
            compare_op=ALU.is_ge, fill=NEG, base=0, pattern=[[-1, 128]], channel_multiplier=1),
            [t_g], s_g)
        t_mask = put("gpsimd", lambda e: e.affine_select(out=mask_k[:, :], in_=mask_k[:, :],
            compare_op=ALU.is_ge, fill=NEG, base=0, pattern=[[1, 128]], channel_multiplier=-1),
            [t_g], s_g)

        s_st = sem("s_st")
        s_pw = sem("s_pw")

        def norm_scale(tiles, ready):
            for i, a in enumerate(tiles):
                t = put("vector", lambda e, i=i, a=a: e.bn_stats(stats[:, i, :], a), ready, s_st)
            for i in range(4):
                t1 = put("vector", lambda e, i=i: e.bn_aggr(mv[:, i, :], stats[:, i, :]), [t], s_st)
            t2 = put("vector", lambda e: e.tensor_scalar(ve[:, :], mv[:, :, 0:2].rearrange(
                "p i c -> p c i")[:, 1, :], EPS, None, ALU.add), [t1], s_st)
            return put("gpsimd", lambda e: e.tensor_tensor(rstd[:, :], ve[:, :], half[:, :],
                       ALU.pow), [t2], s_pw)

        def cut(buf):
            o = buf * 9216
            v = r4[:, o:o + 9216]
            return dict(
                X=v[:, 0:1024].rearrange("p (i d) -> p i d", i=4),
                XT=v[:, 1024:2048].rearrange("p (k t) -> p k t", k=2),
                T0=v[:, 2048:4096].rearrange("p (f t) -> p f t", f=4),
                R=v[:, 4096:6144].rearrange("p (f t) -> p f t", f=4),
                TP=[v[:, 6144 + 1024 * i:7168 + 1024 * i].bitcast(BF)
                    .rearrange("p (f t) -> p f t", f=4) for i in range(3)])

        bufs = [cut(0), cut(1)]
        s_x = [sem("s_x0"), sem("s_x1")]
        s_xn = sem("s_xn")
        s_tr = sem("s_tr")
        s_xt = sem("s_xt")
        s_qk = sem("s_qk")
        s_t0 = sem("s_t0")
        s_pt = sem("s_pt")
        s_v = sem("s_v")
        s_ve = sem("s_ve")
        s_scr = sem("s_scr")
        s_ksl = [sem(f"s_k{g}") for g in range(NG)]
        s_ql = [sem(f"s_q{s}") for s in range(SLOTS)]
        xn_done, parts_done, scr_done, xt_done, t_pv = {}, {}, {}, {}, {}
        bank_free = [t_c] * 8
        scr_sems = [sem("s_scr0"), sem("s_scr1")]
        xload = {}

        def load_x(c):
            b = bufs[c % 2]
            xload[c] = put("sync", Dma(b["X"], x[c * CW:(c + 1) * CW, :].rearrange(
                "(i p) d -> p i d", p=128)), [xn_free.get(c - 2)], s_x[c % 2])

        xn_free = {}

        def load_k(g, c, wait):
            last = None
            for i in range(6):
                last = put("sync", Dma(
                    KS[16 * i:16 * i + 16, g % 2, :, c * CW:(c + 1) * CW],
                    scr[KPART[i], D + 64 * g:D + 64 * g + 64, c * CW:(c + 1) * CW].rearrange(
                        "(h d) t -> d h t", d=HD)), wait, s_ksl[g])
            return last

        kload = {}
        load_x(0)
        load_x(1)
        for c in range(NC):
            b = bufs[c % 2]
            t_r = norm_scale([b["X"][:, i, :] for i in range(4)], [xload[c]])
            for i in range(4):
                t_xn = put("vector", lambda e, b=b, i=i: e.tensor_scalar(
                    b["X"][:, i, :], b["X"][:, i, :], mv[:, i, 0:1], rstd[:, i:i + 1],
                    ALU.subtract, ALU.mult), [t_r], s_xn)
            for k in range(2):
                for i in range(4):
                    t_tr = put("tensor", lambda e, b=b, k=k, i=i: e.transpose(
                        ps[:, k, 128 * i:128 * i + 128], b["X"][:, i, 128 * k:128 * k + 128],
                        idf[:, :]), [t_xn, bank_free[k], t_id], s_tr)
            xn_free[c] = t_tr
            for k in range(2):
                t_xt = put("scalar", lambda e, b=b, k=k: e.copy(b["XT"][:, k, :], ps[:, k, :]),
                           [t_tr, t_pv.get(c - 2)], s_xt)
                bank_free[k] = t_xt
            if c + 2 < NC:
                load_x(c + 2)
            for f in range(4):
                for k in range(2):
                    t_qk = put("tensor", lambda e, b=b, f=f, k=k: e.matmul(
                        ps[:, 2 + f % 2, :], wa[:, k, 128 * f:128 * f + 128], b["XT"][:, k, :],
                        start=(k == 0), stop=(k == 1)), [t_xt, t_w, bank_free[2 + f % 2]],
                        s_qk if k else None)
                t_t0 = put("scalar", lambda e, b=b, f=f: e.activation(
                    b["T0"][:, f, :], ps[:, 2 + f % 2, :], ACT.Identity, bias=ba[:, f:f + 1]),
                    [t_qk, parts_done.get(c - 2)], s_t0)
                bank_free[2 + f % 2] = t_t0
                put("vector", lambda e, b=b, f=f: e.tensor_copy(
                    b["TP"][0][:, f, :], b["T0"][:, f, :]), [t_t0, scr_done.get(c - 2)], s_pt)
            for i in range(4):
                for k in range(2):
                    t_v = put("tensor", lambda e, b=b, i=i, k=k: e.matmul(
                        ps[:, 4 + i % 2, 0:D], b["XT"][:, k, 128 * i:128 * i + 128],
                        wa[:, k, 2 * D:3 * D], start=(k == 0), stop=(k == 1)),
                        [bank_free[4 + i % 2]], s_v if k else None)
                bank_free[4 + i % 2] = put("vector", lambda e, c=c, i=i: e.tensor_tensor(
                    V[:, 4 * c + i, :, 0:HD], ps[:, 4 + i % 2, 0:D].rearrange(
                        "p (h d) -> p h d", h=H), bv[:, :].rearrange("p (h d) -> p h d", h=H),
                    ALU.add), [t_v, t_w], s_ve)
            t_pv[c] = t_v
            t_a = (s_pt, s_pt.n)
            for f in range(4):
                t_b = put("vector", lambda e, b=b, f=f: e.tensor_tensor(
                    b["R"][:, f, :], b["T0"][:, f, :], b["TP"][0][:, f, :], ALU.subtract),
                    [t_a], s_pt)
            for f in range(4):
                t_d = put("vector", lambda e, b=b, f=f: e.tensor_copy(
                    b["TP"][1][:, f, :], b["R"][:, f, :]), [t_b], s_pt)
            for f in range(4):
                parts_done[c] = put("vector", lambda e, b=b, f=f: e.tensor_tensor(
                    b["TP"][2][:, f, :], b["R"][:, f, :], b["TP"][1][:, f, :], ALU.subtract),
                    [t_d], s_pt)
            for i in range(3):
                scr_done[c] = put("sync", Dma(
                    scr[i].rearrange("(f p) t -> p f t", p=128)[:, :, c * CW:(c + 1) * CW],
                    b["TP"][i]), [t_a, parts_done[c]], scr_sems[c % 2])
            kload[0, c] = (0, [scr_done[c]])
        for g in range(2):
            for c in range(NC):
                t_k = load_k(g, c, [scr_done[c]])
            kload[g] = t_k

        units = []
        for g in range(NG):
            order = range(NC) if g % 2 == 0 else range(NC - 1, -1, -1)
            units += [(g, c) for c in order]
        s_ap = sem("s_ap")
        s_mx = sem("s_mx")
        s_mt = sem("s_mt")
        s_ms = sem("s_ms")
        s_mw = [sem("s_mw0"), sem("s_mw1")]
        s_mr = [sem(f"s_mr{s}") for s in range(SLOTS)]
        s_sT = sem("s_sT")
        s_ex = sem("s_ex")
        s_pv = sem("s_pv")
        s_oc = sem("s_oc")
        s_os = [sem("s_os0"), sem("s_os1")]
        OB = r4[:, 17408:18432].rearrange("p (b t) -> p b t", b=2)
        qload, mload, st_done, os_done = {}, {}, {}, {}
        ms_done, mw_done = {}, {}
        ap_free = [bank_free[4], bank_free[5]]
        st_free = [[bank_free[0], bank_free[1]], [bank_free[2], bank_free[3]]]
        pb_free = [None] * 4
        o_free = [t_c, t_c]
        npiece = 0
        scr_all = [scr_done[NC - 2], scr_done[NC - 1]]

        def load_q(u):
            g, c = units[u]
            s = u % SLOTS
            for i in range(6):
                qload[u] = put("sync", Dma(
                    QS[16 * i:16 * i + 16, s, :, :],
                    scr[QPART[i], 64 * g:64 * g + 64, c * CW:(c + 1) * CW].rearrange(
                        "(h d) t -> d h t", d=HD)), [*scr_all, st_done.get(u - SLOTS)], s_ql[s])

        def piece(u, h, qt, k):
            nonlocal npiece
            g, c = units[u]
            b = npiece % 2
            npiece += 1
            n = CW if k < c else 128 * (qt + 1)
            bank = ps[:, 4 + b, :]
            lhs = QS[0:ROWS, u % SLOTS, h, 128 * qt:128 * qt + 128]
            rhs = KS[0:ROWS, g % 2, h, CW * k:CW * k + n]
            diag = k == c
            t = put("tensor", lambda e: e.matmul(bank[:, 0:n], lhs, rhs, start=True,
                    stop=not diag), [ap_free[b], qload[u], kload[g], *scr_all],
                    None if diag else s_ap)
            if diag:
                t = put("tensor", lambda e: e.matmul(bank[:, n - 128:n], idb[:, :], mask_q[:, :],
                        start=False, stop=True), [t_mask, t_c], s_ap)
            dst = mp[:, u % 2, 4 * h + qt, k:k + 1]
            ap_free[b] = put("vector", lambda e: e.tensor_reduce(dst, bank[:, 0:n], AX.X, ALU.max),
                             [t], s_mx)

        def row_max(u):
            nonlocal npiece
            g, c = units[u]
            b = npiece % 2
            npiece += 1
            bank = ps[:, 4 + b, :]
            t = put("vector", lambda e: e.tensor_reduce(mm[:, :], mp[:, u % 2, :, 0:c + 1], AX.X,
                    ALU.max), [(s_mx, s_mx.n), (s_mt, s_mt.n)], s_ms)
            t = put("tensor", lambda e: e.transpose(bank[0:16, 0:128], mm[:, :], idf[:, :]),
                    [t, ap_free[b]], s_mt)
            t = put("vector", lambda e: e.tensor_scalar(m1[:, 0, :], bank[0:16, 0:128], -1.0, None,
                    ALU.mult), [t, mw_done.get(u - 1)], s_ms)
            t = put("vector", lambda e: e.scalar_tensor_tensor(
                out=mr[:, :], in0=bank[0:16, 0:128], scalar=-1.0, in1=m1[:, 0, :], op0=ALU.mult,
                op1=ALU.subtract), [t], s_ms)
            ap_free[b] = t
            t = put("vector", lambda e: e.tensor_copy(m1[:, 1, :], mr[:, :]), [t], s_ms)
            t = put("vector", lambda e: e.tensor_tensor(m1[:, 2, :], mr[:, :], m1[:, 1, :],
                    ALU.subtract), [t], s_ms)
            mw_done[u] = put("sync", Dma(mscr[u].rearrange("i (p q) -> p i q", q=128), m1[:, :, :]),
                             [t], s_mw[u % 2])
            s = u % SLOTS
            mload[u] = put("sync", Dma(QS[ROWS:ROWS + 3, s, :, :].rearrange("i h t -> i (h t)"),
                           mscr[u]), [mw_done[u], st_done.get(u - SLOTS)], s_mr[s])

        nst = 0

        def scores(u, kt, pair):
            nonlocal nst
            g, c = units[u]
            off = 128 * max(0, kt - 4 * c)
            b = nst % 2
            pb = nst % 4
            nst += 1
            for hh in range(2):
                h = 2 * pair + hh
                bank = ps[:, 2 * b + hh, :]
                diag = kt >= 4 * c
                lhs = KS[0:ROWS + 3, g % 2, h, 128 * kt:128 * kt + 128]
                rhs = QS[0:ROWS + 3, u % SLOTS, h, off:CW]
                t = put("tensor", lambda e, bank=bank, lhs=lhs, rhs=rhs: e.matmul(
                    bank[:, off:CW], lhs, rhs, start=True, stop=not diag),
                    [*st_free[b], mload[u], qload[u], kload[g]], None if diag else s_sT)
                if diag:
                    t = put("tensor", lambda e, bank=bank: e.matmul(
                        bank[:, off:off + 128], idb[:, :], mask_k[:, :], start=False, stop=True),
                        [t_mask], s_sT)
            st_done[u] = t
            t = put("scalar", lambda e: e.activation(PB[:, pb, :, off:CW],
                    ps[:, 2 * b:2 * b + 2, off:CW], ACT.Exp, scale=HD ** -0.5),
                    [t, pb_free[pb]], s_ex)
            st_free[b] = [t]
            return t, pb

        def values(u, kt, done):
            g, c = units[u]
            off = 128 * max(0, kt - 4 * c)
            o = ps[:, 6 + u % 2, :]
            for h in range(GH):
                ex, pb = done[h // 2]
                t = put("tensor", lambda e, h=h, pb=pb: e.matmul(
                    o[32 * h:32 * h + HD + 1, off:CW], V[:, kt, GH * g + h, :],
                    PB[:, pb, h % 2, off:CW], start=(kt == 0), stop=(kt == 4 * c + 3),
                    tile_position=(0, 32 * h)), [ex, o_free[u % 2]],
                    s_pv if h % 2 else None)
                if h % 2:
                    pb_free[pb] = t
            return t

        def flush(u, t):
            g, c = units[u]
            ob = OB[:, u % 2, :]
            t = put("scalar", lambda e: e.copy(ob, ps[:, 6 + u % 2, :]),
                    [t, *os_done.get(u - 2, [])], s_oc)
            o_free[u % 2] = t
            for h in range(GH):
                put("sync", Dma(oscr[16 * (GH * g + h):16 * (GH * g + h) + 16,
                                     c * CW:(c + 1) * CW], ob[32 * h:32 * h + 16, :]),
                    [t], s_os[u % 2])
                z = put("sync", Dma(dscr[GH * g + h:GH * g + h + 1, c * CW:(c + 1) * CW],
                                    ob[32 * h + 16:32 * h + 17, :]), [t], s_os[u % 2])
            os_done[u] = [z]

        load_q(0)
        load_q(1)
        late = None
        prev = None
        for n in range(len(units) + 2):
            if 0 < n and n + 1 < len(units):
                load_q(n + 1)
            if n % 8 == 3 and n + 5 < len(units) and (n + 5) // 8 >= 2:
                g = (n + 5) // 8
                for c in range(NC):
                    kload[g] = load_k(g, c, [st_done[8 * (g - 1) - 1], *scr_all])
            todo = []
            if n < len(units):
                c = units[n][1]
                todo = [(n, h, qt, k) for h in range(GH) for qt in range(4) for k in range(c + 1)]
            steps = 0
            if n >= 2:
                steps = 4 * units[n - 2][1] + 4
            at = 0
            for kt in range(steps):
                upto = len(todo) * (kt + 1) // steps
                mid = (at + upto) // 2
                d0 = scores(n - 2, kt, 0)
                for p in todo[at:mid]:
                    piece(*p)
                d1 = scores(n - 2, kt, 1)
                for p in todo[mid:upto]:
                    piece(*p)
                at = upto
                if late is not None:
                    t_last = values(*late)
                    if late[1] == 4 * units[late[0]][1] + 3:
                        flush(late[0], t_last)
                late = (n - 2, kt, [d0, d1])
            for p in todo[at:]:
                piece(*p)
            if n < len(units):
                row_max(n)
        t_last = values(*late)
        flush(late[0], t_last)
        u_last = len(units) - 1
        attn = [*os_done[u_last - 1], *os_done[u_last]]
        pe_end = t_last

        W1 = r4[:, 0:2048].rearrange("p (k n) -> p k n", k=2)
        W2 = r4[:, 2048:4096].rearrange("p (k n) -> p k n", k=2)
        H1 = r4[:, 4096:12288].rearrange("p (k n) -> p k n", k=8)
        W3 = r4[:, 12288:14336].rearrange("p (k n) -> p k n", k=8)
        WP = r4[:, 14336:14848].rearrange("p (k n) -> p k n", k=2)
        S1 = r4[:, 14848:14856]
        S2 = r4[:, 14856:14864]
        G1 = r4[:, 14864:14872]
        G2 = r4[:, 14872:14880]
        BP = r4[:, 14880:15136]
        S3 = r4[:, 15136:15392]
        H2 = r1[:, 0:8192].rearrange("p (k n) -> p k n", k=8)
        XX = [r1[:, 8192 + 1024 * b:9216 + 1024 * b].rearrange("p (i d) -> p i d", i=4)
              for b in range(2)]
        YY = r1[:, 10240:11264].rearrange("p (i d) -> p i d", i=4)
        XT = [r1[:, 11264 + 1024 * b:12288 + 1024 * b].rearrange("p (k t) -> p k t", k=2)
              for b in range(2)]
        OT = r1[:, 13312:14336].rearrange("p (k t) -> p k t", k=2)
        DN = r1[:, 14336:15360].rearrange("p (k t) -> p k t", k=2)
        SG = [r1[:, 15360 + 512 * b:15872 + 512 * b] for b in range(2)]
        HA = r2[:, 0:4096].rearrange("p (k t) -> p k t", k=8)
        HB = r2[:, 4096:8192].rearrange("p (k t) -> p k t", k=8)
        ZZ = V[:, :, :, :].rearrange("p a b c -> p (a b c)")[:, 0:1024].rearrange(
            "p (i d) -> p i d", i=4)

        s_wl = sem("s_wl")
        free4 = [scr_all[0], scr_all[1], parts_done[NC - 1], (s_tr, s_tr.n), t_pv[NC - 1]]
        for dst, src in ((W1, w1t), (W2, w2t), (H1, h1t), (W3, w3t), (WP, w_proj)):
            put("sync", Dma(dst, src.rearrange("(k p) n -> p k n", p=128)), free4, s_wl)
        for dst, src in ((S1, w1_s), (S2, w2_s), (G1, h1_s), (G2, h2_s)):
            put("sync", Dma(dst, src), free4, s_wl)
        for dst, src in ((BP, b_proj), (S3, w3_s)):
            t_wl = put("sync", Dma(dst, src.rearrange("(a n) -> a n", a=1)
                                   .to_broadcast([128, D])), free4, s_wl)
        s_h2 = sem("s_h2")
        t_h2 = put("sync", Dma(H2, h2t.rearrange("(k p) n -> p k n", p=128)), [pe_end], s_h2)

        s_in = [sem("s_in0"), sem("s_in1")]
        s_on = sem("s_on")
        s_pj = sem("s_pj")
        s_y = sem("s_y")
        s_x1 = sem("s_res")
        s_t3 = sem("s_t3")
        s_c3 = sem("s_c3")
        s_mm = sem("s_mm")
        s_sg = sem("s_sg")
        s_ha = sem("s_ha")
        s_hb = sem("s_hb")
        s_hc = sem("s_hc")
        s_l4 = sem("s_l4")
        s_z = sem("s_z")
        s_out = [sem("s_o0"), sem("s_o1")]
        last_exp = (s_ex, s_ex.n)
        fin = (s_oc, s_oc.n)
        bank = {b: [last_exp, fin, ap_free[0], ap_free[1], pe_end] for b in range(8)}
        on_done, pj_done, y_free, t3_done, l1_done, out_done = {}, {}, {}, {}, {}, {}
        ot_free = [pe_end]
        in_done = {}

        def load_in(c):
            for k in range(2):
                put("sync", Dma(OT[:, k, :], oscr[128 * k:128 * k + 128, c * CW:(c + 1) * CW]),
                    [*attn, pe_end, pj_done.get(c - 1)], s_in[c % 2])
                for h in range(8):
                    put("sync", Dma(DN[16 * h:16 * h + 16, k, :],
                                    dscr[8 * k + h:8 * k + h + 1, c * CW:(c + 1) * CW]
                                    .to_broadcast([16, CW])), [on_done.get(c - 1)], s_in[c % 2])
            in_done[c] = put("sync", Dma(XX[c % 2], x[c * CW:(c + 1) * CW, :].rearrange(
                "(i p) d -> p i d", p=128)), [out_done.get(c - 2)], s_in[c % 2])

        def front_a(c):
            X, Y = XX[c % 2], YY
            t = put("vector", lambda e: e.reciprocal(DN, DN), [in_done[c]], s_on)
            on_done[c] = t = put("vector", lambda e: e.tensor_tensor(OT, OT, DN, ALU.mult), [t], s_on)
            for i in range(4):
                b = 4 + i % 2
                for k in range(2):
                    tp = put("tensor", lambda e, b=b, i=i, k=k: e.matmul(
                        ps[:, b, 0:D], OT[:, k, 128 * i:128 * i + 128], WP[:, k, :],
                        start=(k == 0), stop=(k == 1)), [t, t_wl, *bank[b]], s_pj if k else None)
                ty = put("vector", lambda e, b=b, i=i: e.tensor_tensor(
                    Y[:, i, :], ps[:, b, 0:D], BP, ALU.add), [tp, t3_done.get(c - 1)], s_y)
                bank[b] = [ty]
            pj_done[c] = tp
            tr = norm_scale([Y[:, i, :] for i in range(4)], [ty])
            for i in range(4):
                t = put("vector", lambda e, i=i: e.tensor_scalar(
                    Y[:, i, :], Y[:, i, :], mv[:, i, 0:1], rstd[:, i:i + 1], ALU.subtract,
                    ALU.mult), [tr], s_y)
            t = put("vector", lambda e: e.tensor_tensor(X, X, Y, ALU.add), [t], s_x1)
            tr = norm_scale([X[:, i, :] for i in range(4)], [t])
            for i in range(4):
                t = put("vector", lambda e, i=i: e.tensor_scalar(
                    Y[:, i, :], X[:, i, :], mv[:, i, 0:1], rstd[:, i:i + 1], ALU.subtract,
                    ALU.mult), [tr], s_y)
            y_free[c] = t

        xt3 = {}

        def front_b(c):
            for k in range(2):
                for i in range(4):
                    t = put("tensor", lambda e, k=k, i=i: e.transpose(
                        ps[:, 6 + k, 128 * i:128 * i + 128], YY[:, i, 128 * k:128 * k + 128],
                        idf[:, :]), [y_free[c], *bank[6 + k]], s_t3)
                tc = put("vector", lambda e, k=k: e.tensor_copy(XT[c % 2][:, k, :], ps[:, 6 + k, :]),
                         [t, l1_done.get(c - 2)], s_c3)
                bank[6 + k] = [tc]
            t3_done[c] = t
            xt3[c] = tc

        rot = 0
        sg_free = [None, None]
        hb_free, ha_free = None, None

        def product(lhs, rhs, nk, wait):
            nonlocal rot
            b = rot % 4
            rot += 1
            for k in range(nk):
                t = put("tensor", lambda e, k=k, l=lhs(k), r=rhs(k): e.matmul(ps[:, b, :], l, r,
                        start=(k == 0), stop=(k == nk - 1)), [*wait(k), *bank[b]],
                        s_mm if k == nk - 1 else None)
            return b, t

        def layer1(c):
            done = []
            for m in range(8):
                ms = slice(128 * m, 128 * m + 128)
                ba_, ta = product(lambda k: W1[:, k, ms], lambda k: XT[c % 2][:, k, :], 2,
                                  lambda k: [xt3[c], t_wl])
                bb_, tb = product(lambda k: W2[:, k, ms], lambda k: XT[c % 2][:, k, :], 2,
                                  lambda k: [xt3[c], t_wl])
                q = m % 2
                ts = put("scalar", lambda e, q=q, b=ba_, m=m: e.activation(
                    SG[q], ps[:, b, :], ACT.Silu, scale=S1[:, m:m + 1]), [ta, sg_free[q]], s_sg)
                bank[ba_] = [ts]
                tv = put("vector", lambda e, q=q, b=bb_, m=m: e.scalar_tensor_tensor(
                    out=HA[:, m, :], in0=ps[:, b, :], scalar=S2[:, m:m + 1], in1=SG[q],
                    op0=ALU.mult, op1=ALU.mult), [ts, tb, ha_free], s_ha)
                bank[bb_] = [tv]
                sg_free[q] = tv
                done.append(tv)
            l1_done[c] = tb
            return done

        def layer(W, S, src, dst, ready, free, s):
            done = []
            for m in range(8):
                ms = slice(128 * m, 128 * m + 128)
                b, t = product(lambda k: W[:, k, ms], lambda k: src[:, k, :], 8,
                               lambda k: [ready[k], t_wl, t_h2])
                tg = put("scalar", lambda e, b=b, m=m: e.activation(
                    dst[:, m, :], ps[:, b, :], ACT.Gelu, scale=S[:, m:m + 1]), [t, free], s)
                bank[b] = [tg]
                done.append(tg)
            return done, t

        def layer4(c, ready):
            X = XX[c % 2]
            for i in range(4):
                b = 4 + i % 2
                for k in range(8):
                    t = put("tensor", lambda e, b=b, i=i, k=k: e.matmul(
                        ps[:, b, 0:D], HA[:, k, 128 * i:128 * i + 128], W3[:, k, :],
                        start=(k == 0), stop=(k == 7)), [ready[k], *bank[b]],
                        s_l4 if k == 7 else None)
                tz = put("vector", lambda e, b=b, i=i: e.tensor_tensor(
                    ZZ[:, i, :], ps[:, b, 0:D], S3, ALU.mult), [t], s_z)
                bank[b] = [tz]
            tr = norm_scale([ZZ[:, i, :] for i in range(4)], [tz])
            for i in range(4):
                tz = put("vector", lambda e, i=i: e.tensor_scalar(
                    ZZ[:, i, :], ZZ[:, i, :], mv[:, i, 0:1], rstd[:, i:i + 1], ALU.subtract,
                    ALU.mult), [tr], s_z)
            tz = put("vector", lambda e: e.tensor_tensor(X, X, ZZ, ALU.add), [tz], s_z)
            out_done[c] = put("sync", Dma(out[c * CW:(c + 1) * CW, :].rearrange(
                "(i p) d -> p i d", p=128), X), [tz], s_out[c % 2])
            return t

        load_in(0)
        front_a(0)
        front_b(0)
        if NC > 1:
            load_in(1)
        for c in range(NC):
            r = layer1(c)
            if c + 1 < NC:
                front_a(c + 1)
            r, hap = layer(H1, G1, HA, HB, r, hb_free, s_hb)
            r, hbp = layer(H2, G2, HB, HA, r, hap, s_hc)
            hb_free = hbp
            if c + 1 < NC:
                front_b(c + 1)
            ha_free = layer4(c, r)
            if c + 2 < NC:
                load_in(c + 2)
        put("sync", lambda e: e.nop(), [out_done[NC - 2], out_done[NC - 1]])

        block = ctx.enter_context(nc.Block())

        @block.sync
        def _(e):
            P.run("sync", e)

        @block.tensor
        def _(e):
            P.run("tensor", e)

        @block.vector
        def _(e):
            P.run("vector", e)

        @block.scalar
        def _(e):
            P.run("scalar", e)

        @block.gpsimd
        def _(e):
            P.run("gpsimd", e)


def kernel(**inputs):
    import numpy as np
    import concourse.bacc as bacc
    from concourse import mybir as mb
    from concourse.bass_utils import run_bass_kernel_spmd as run

    def a(name):
        return np.asarray(inputs[name])

    def columns(v):
        return v.reshape(-1, 128).T

    arrays = {
        "x": a("L0_attn_x").reshape(T, D),
        "w_attn": a("L0_attn_w_attn"), "b_attn": a("L0_attn_b_attn"),
        "b_qk": columns(a("L0_attn_b_attn")[0:2 * D]),
        "w_proj": a("L0_attn_w_proj"), "b_proj": a("L0_attn_b_proj"),
        "w1t": a("L0_ffn_w1_w").T, "w1_s": columns(a("L0_ffn_w1_s")),
        "w2t": a("L0_ffn_w2_w").T, "w2_s": columns(a("L0_ffn_w2_s")),
        "h1t": a("L0_ffn_h1_w").T, "h1_s": columns(a("L0_ffn_h1_s")),
        "h2t": a("L0_ffn_h2_w").T, "h2_s": columns(a("L0_ffn_h2_s")),
        "w3t": a("L0_ffn_w3_w").T, "w3_s": a("L0_ffn_w3_s"),
        "ident": np.eye(128, dtype=np.float32),
    }
    arrays = {f"in_{k}": np.ascontiguousarray(v) for k, v in arrays.items()}
    nc = bacc.Bacc("TRN2", target_bir_lowering=False, num_devices=1)
    args = [nc.dram_tensor(k, v.shape, mb.dt.from_np(v.dtype), kind="ExternalInput").ap()
            for k, v in arrays.items()]
    out = nc.dram_tensor("out_0", (T, D), F32, kind="ExternalOutput").ap()
    build(nc, *args, out)
    r = run(nc, [arrays], core_ids=[0])
    return r.results[0]["out_0"].reshape(1, T, D)
```

```python
from contextlib import ExitStack

import concourse.bass as bass
from concourse import mybir

F32 = mybir.dt.float32
BF = mybir.dt.bfloat16
FR = mybir.dt.float32r
I32 = mybir.dt.int32
ALU = mybir.AluOpType
ACT = mybir.ActivationFunctionType
AX = mybir.AxisListType

T = 4096
D = 256
H = 16
HD = 16
F = 1024
CW = 512
NC = T // CW
GH = 4
NG = H // GH
SLOTS = 4
PBN = 8
STB = [0, 1, 2]
MXB = [3, 4, 5]
OUB = [6, 7]
MARGIN = 3
NEG = -1.0e30
EPS = 1e-5
KPART = [0, 0, 1, 0, 2, 1]
QPART = [0, 1, 0, 2, 0, 1]
ROWS = 96


class Count:

    def __init__(self, handle):
        self.handle = handle
        self.n = 0


class Program:

    def __init__(self):
        self.queues = {k: [] for k in ("sync", "tensor", "vector", "scalar", "gpsimd")}
        self.turn = None

    def put(self, engine, make, wait=(), inc=None, general=False):
        wait = [w for w in wait if w is not None]
        step = None
        if inc is not None:
            step = 16 if engine == "sync" or isinstance(make, Dma) else 1
            inc.n += step
        self.queues[engine].append((make, wait, inc, step, general))
        return (inc, inc.n) if inc is not None else None

    def branch(self, flag, ready):
        self.turn = {k: len(q) for k, q in self.queues.items()}
        self.flag, self.flag_ready = flag, ready

    def run(self, engine, e):
        queue = self.queues[engine]
        n = self.turn[engine]
        self.emit(e, queue[:n], {})
        if any(q[4] for q in queue[n:]):
            sem, value = self.flag_ready
            e.wait_ge(sem.handle, value)
            flag = e.value_load(self.flag)
            with e.If(flag != 0):
                self.emit(e, queue[n:], {})
            with e.Else():
                self.emit(e, [q for q in queue[n:] if not q[4]], {})
        else:
            self.emit(e, queue[n:], {})

    def emit(self, e, queue, reached):
        for make, wait, inc, step, _ in queue:
            for sem, value in wait:
                if reached.get(id(sem), 0) < value:
                    e.wait_ge(sem.handle, value)
                    reached[id(sem)] = value
            ins = make(e)
            if inc is not None:
                ins.then_inc(inc.handle, step)


class Dma:
    def __init__(self, dst, src):
        self.dst, self.src = (a.bitcast(F32) if a.dtype == FR else a for a in (dst, src))

    def __call__(self, e):
        return e.dma_start(self.dst, self.src)


def build(nc, x, w_attn, b_attn, b_qk, w_proj, b_proj, w1t, w1_s, w2t, w2_s, h1t, h1_s, h2t, h2_s,
          w3t, w3_s, ident, out):
    scr = nc.dram_tensor("qk_parts", (3, 2 * D, T), BF, kind="Internal").ap()
    mscr = nc.dram_tensor("row_max", (NG * NC, 3, GH * CW), BF, kind="Internal").ap()
    oscr = nc.dram_tensor("attn_out", (D, T), F32, kind="Internal").ap()
    dscr = nc.dram_tensor("attn_den", (H, T), F32, kind="Internal").ap()

    ctx = ExitStack()
    with ctx:
        def sb(name, shape, dt=F32):
            return ctx.enter_context(nc.sbuf_tensor(name, shape, dt))

        def sem(name):
            return Count(ctx.enter_context(nc.semaphore(name)))

        base = -(-nc.sbuf_base // 32) * 32
        sb("area", [128, 18432 + 16384 + 8192 + 8704])

        def at(name, first, n, dt=F32):
            return nc.alloc_sbuf_tensor_at(name, [128, n], dt, offset=base + 4 * first)

        A0, A1, A2, A3 = 0, 18432, 18432 + 16384, 18432 + 16384 + 8192
        r4 = at("r4", A0, 18432)
        r1 = at("r1", A1, 16384)
        r2 = at("r2", A2, 8192)
        V = at("V", A3, 8704)[:, :].rearrange("p (t h d) -> p t h d", t=T // 128, h=H)
        wres = at("wres", A0, 14336, FR)
        tail = at("tail", A0 + 14336, 3072)
        wst = at("wst", A0 + 14336 + 3072, 1024, FR)
        h2r = at("h2r", A1, 8192, FR)
        hbr = at("hbr", A1 + 8192, 8192, FR)
        har = at("har", A2, 8192, FR)
        xtr = at("xtr", A3, 4096, FR)
        late3 = at("late3", A3 + 4096, 4608)
        wlr = at("wlr", A0 + 14336 + 3072, 1024, FR)
        acc = sb("acc", [128, 44])
        accs = sb("accs", [128, 1])
        one = sb("one", [128, 1])
        flag = sb("flag", [1, 1])
        idf = sb("idf", [128, 128])
        idb = sb("idb", [128, 128], BF)
        mask_q = sb("mask_q", [128, 128], BF)
        mask_k = sb("mask_k", [128, 128], BF)
        wa = r2[:, 4096:5632].rearrange("p (k n) -> p k n", k=2)
        ba = sb("ba", [128, 4])
        bv = sb("bv", [128, D])
        stats = sb("stats", [128, 4, 6])
        mv = sb("mv", [128, 4, 2])
        ve = sb("ve", [128, 4])
        rstd = sb("rstd", [128, 4])
        half = sb("half", [128, 4])
        mp = sb("mp", [128, 2, 16, NC], F32)
        mm = sb("mm", [128, 16])
        m1 = sb("m1", [16, 3, 128], BF)
        mr = sb("mr", [16, 128])
        ps = ctx.enter_context(nc.psum_tensor("ps", [128, 8, 512], F32))

        KS = r1[:, :].bitcast(BF).rearrange("p (b h t) -> p b h t", b=2, h=GH)
        QS = r2[:, 0:4096].bitcast(BF).rearrange("p (s h t) -> p s h t", s=SLOTS, h=GH)
        PB = r2[:, 4096:8192].rearrange("p (n t) -> p n t", n=PBN)

        P = Program()
        put = P.put

        s_ld = sem("s_ld")
        s_id = sem("s_id")
        s_c = sem("s_c")
        t_id = put("sync", Dma(idf[:, :], ident), inc=s_id)
        s_w = sem("s_w")
        put("sync", Dma(wa, w_attn.rearrange("(k p) n -> p k n", p=128)), inc=s_w)
        put("sync", Dma(ba[:, :], b_qk), inc=s_w)
        t_w = put("sync", Dma(bv[:, :], b_attn[2 * D:3 * D].rearrange("(a n) -> a n", a=1)
                              .to_broadcast([128, D])), inc=s_w)
        put("vector", lambda e: e.memset(half[:, :], -0.5), inc=s_c)
        put("vector", lambda e: e.memset(one[:, :], 1.0), inc=s_c)
        put("vector", lambda e: e.memset(V[:, :, :, HD:HD + 1], 1.0), inc=s_c)
        put("vector", lambda e: e.memset(ps[:, 6:8, :], 0.0), inc=s_c)
        for b in range(2):
            put("vector", lambda e, b=b: e.memset(KS[ROWS:ROWS + 3, b, :, :], 1.0), inc=s_c)
        t_c = put("vector", lambda e: e.tensor_copy(idb[:, :], idf[:, :]), [t_id], s_c)
        s_g = sem("s_g")
        put("gpsimd", lambda e: e.memset(mask_q[:, :], 0.0), inc=s_g)
        t_g = put("gpsimd", lambda e: e.memset(mask_k[:, :], 0.0), inc=s_g)
        put("gpsimd", lambda e: e.affine_select(out=mask_q[:, :], in_=mask_q[:, :],
            compare_op=ALU.is_ge, fill=NEG, base=0, pattern=[[-1, 128]], channel_multiplier=1),
            [t_g], s_g)
        t_mask = put("gpsimd", lambda e: e.affine_select(out=mask_k[:, :], in_=mask_k[:, :],
            compare_op=ALU.is_ge, fill=NEG, base=0, pattern=[[1, 128]], channel_multiplier=-1),
            [t_g], s_g)

        s_st = sem("s_st")
        s_pw = sem("s_pw")

        def norm_scale(tiles, ready):
            for i, a in enumerate(tiles):
                t = put("vector", lambda e, i=i, a=a: e.bn_stats(stats[:, i, :], a), ready, s_st)
            for i in range(4):
                t1 = put("vector", lambda e, i=i: e.bn_aggr(mv[:, i, :], stats[:, i, :]), [t], s_st)
            t2 = put("vector", lambda e: e.tensor_scalar(ve[:, :], mv[:, :, 0:2].rearrange(
                "p i c -> p c i")[:, 1, :], EPS, None, ALU.add), [t1], s_st)
            return put("gpsimd", lambda e: e.tensor_tensor(rstd[:, :], ve[:, :], half[:, :],
                       ALU.pow), [t2], s_pw)

        def cut(buf):
            o = buf * 9216
            v = r4[:, o:o + 9216]
            return dict(
                X=v[:, 0:1024].rearrange("p (i d) -> p i d", i=4),
                XT=v[:, 1024:2048].rearrange("p (k t) -> p k t", k=2),
                T0=v[:, 2048:4096].rearrange("p (f t) -> p f t", f=4),
                R=v[:, 4096:6144].rearrange("p (f t) -> p f t", f=4),
                TP=[v[:, 6144 + 1024 * i:7168 + 1024 * i].bitcast(BF)
                    .rearrange("p (f t) -> p f t", f=4) for i in range(3)])

        bufs = [cut(0), cut(1)]
        s_x = [sem("s_x0"), sem("s_x1")]
        s_xn = sem("s_xn")
        s_tr = sem("s_tr")
        s_xt = sem("s_xt")
        s_qk = sem("s_qk")
        s_t0 = sem("s_t0")
        s_pt = sem("s_pt")
        s_v = sem("s_v")
        s_ve = sem("s_ve")
        s_scr = sem("s_scr")
        s_ksl = [sem(f"s_k{g}") for g in range(NG)]
        s_ql = [sem(f"s_q{s}") for s in range(SLOTS)]
        xn_done, parts_done, scr_done, xt_done, t_pv = {}, {}, {}, {}, {}
        bank_free = [t_c] * 8
        scr_sems = [sem("s_scr0"), sem("s_scr1")]
        xload = {}

        def load_x(c):
            b = bufs[c % 2]
            xload[c] = put("sync", Dma(b["X"], x[c * CW:(c + 1) * CW, :].rearrange(
                "(i p) d -> p i d", p=128)), [xn_free.get(c - 2)], s_x[c % 2])

        xn_free = {}

        def load_k(g, c, wait):
            last = None
            for i in range(6):
                last = put("sync", Dma(
                    KS[16 * i:16 * i + 16, g % 2, :, c * CW:(c + 1) * CW],
                    scr[KPART[i], D + 64 * g:D + 64 * g + 64, c * CW:(c + 1) * CW].rearrange(
                        "(h d) t -> d h t", d=HD)), wait, s_ksl[g])
            return last

        kload = {}
        load_x(0)
        load_x(1)
        for c in range(NC):
            b = bufs[c % 2]
            t_r = norm_scale([b["X"][:, i, :] for i in range(4)], [xload[c]])
            for i in range(4):
                t_xn = put("vector", lambda e, b=b, i=i: e.tensor_scalar(
                    b["X"][:, i, :], b["X"][:, i, :], mv[:, i, 0:1], rstd[:, i:i + 1],
                    ALU.subtract, ALU.mult), [t_r], s_xn)
            for k in range(2):
                for i in range(4):
                    t_tr = put("tensor", lambda e, b=b, k=k, i=i: e.transpose(
                        ps[:, k, 128 * i:128 * i + 128], b["X"][:, i, 128 * k:128 * k + 128],
                        idf[:, :]), [t_xn, bank_free[k], t_id], s_tr)
            xn_free[c] = t_tr
            for k in range(2):
                t_xt = put("scalar", lambda e, b=b, k=k: e.copy(b["XT"][:, k, :], ps[:, k, :]),
                           [t_tr, t_pv.get(c - 2)], s_xt)
                bank_free[k] = t_xt
            if c + 2 < NC:
                load_x(c + 2)
            for f in range(4):
                for k in range(2):
                    t_qk = put("tensor", lambda e, b=b, f=f, k=k: e.matmul(
                        ps[:, 2 + f % 2, :], wa[:, k, 128 * f:128 * f + 128], b["XT"][:, k, :],
                        start=(k == 0), stop=(k == 1)), [t_xt, t_w, bank_free[2 + f % 2]],
                        s_qk if k else None)
                t_t0 = put("scalar", lambda e, b=b, f=f: e.activation(
                    b["T0"][:, f, :], ps[:, 2 + f % 2, :], ACT.Identity, bias=ba[:, f:f + 1]),
                    [t_qk, parts_done.get(c - 2)], s_t0)
                bank_free[2 + f % 2] = t_t0
                put("vector", lambda e, b=b, f=f: e.tensor_copy(
                    b["TP"][0][:, f, :], b["T0"][:, f, :]), [t_t0, scr_done.get(c - 2)], s_pt)
            for i in range(4):
                for k in range(2):
                    t_v = put("tensor", lambda e, b=b, i=i, k=k: e.matmul(
                        ps[:, 4 + i % 2, 0:D], b["XT"][:, k, 128 * i:128 * i + 128],
                        wa[:, k, 2 * D:3 * D], start=(k == 0), stop=(k == 1)),
                        [bank_free[4 + i % 2]], s_v if k else None)
                bank_free[4 + i % 2] = put("vector", lambda e, c=c, i=i: e.tensor_tensor(
                    V[:, 4 * c + i, :, 0:HD], ps[:, 4 + i % 2, 0:D].rearrange(
                        "p (h d) -> p h d", h=H), bv[:, :].rearrange("p (h d) -> p h d", h=H),
                    ALU.add), [t_v, t_w], s_ve)
            t_pv[c] = t_v
            t_a = (s_pt, s_pt.n)
            for f in range(4):
                t_b = put("vector", lambda e, b=b, f=f: e.tensor_tensor(
                    b["R"][:, f, :], b["T0"][:, f, :], b["TP"][0][:, f, :], ALU.subtract),
                    [t_a], s_pt)
            for f in range(4):
                t_d = put("vector", lambda e, b=b, f=f: e.tensor_copy(
                    b["TP"][1][:, f, :], b["R"][:, f, :]), [t_b], s_pt)
            for f in range(4):
                parts_done[c] = put("vector", lambda e, b=b, f=f: e.tensor_tensor(
                    b["TP"][2][:, f, :], b["R"][:, f, :], b["TP"][1][:, f, :], ALU.subtract),
                    [t_d], s_pt)
            for i in range(3):
                scr_done[c] = put("sync", Dma(
                    scr[i].rearrange("(f p) t -> p f t", p=128)[:, :, c * CW:(c + 1) * CW],
                    b["TP"][i]), [t_a, parts_done[c]], scr_sems[c % 2])
            kload[0, c] = (0, [scr_done[c]])
        for g in range(2):
            for c in range(NC):
                t_k = load_k(g, c, [scr_done[c]])
            kload[g] = t_k

        units = []
        for g in range(NG):
            order = range(NC) if g % 2 == 0 else range(NC - 1, -1, -1)
            units += [(g, c) for c in order]
        s_ap = sem("s_ap")
        s_mx = sem("s_mx")
        s_mt = sem("s_mt")
        s_ms = sem("s_ms")
        s_mw = [sem("s_mw0"), sem("s_mw1")]
        s_mr = [sem(f"s_mr{s}") for s in range(SLOTS)]
        s_sT = sem("s_sT")
        s_ex = sem("s_ex")
        s_pv = sem("s_pv")
        s_oc = sem("s_oc")
        s_os = [sem("s_os0"), sem("s_os1")]
        OB = tail[:, 1024:2048].rearrange("p (b t) -> p b t", b=2)
        qload, mload, st_done, os_done = {}, {}, {}, {}
        ms_done, mw_done = {}, {}
        ap_free = [bank_free[b] for b in MXB]
        st_free = [bank_free[b] for b in STB]
        pb_free = [None] * PBN
        o_free = [t_c, t_c]
        npiece = 0
        scr_all = [scr_done[NC - 2], scr_done[NC - 1]]

        def load_q(u):
            g, c = units[u]
            s = u % SLOTS
            for i in range(6):
                qload[u] = put("sync", Dma(
                    QS[16 * i:16 * i + 16, s, :, :],
                    scr[QPART[i], 64 * g:64 * g + 64, c * CW:(c + 1) * CW].rearrange(
                        "(h d) t -> d h t", d=HD)), [*scr_all, st_done.get(u - SLOTS)], s_ql[s])

        def piece(u, h, qt, k):
            nonlocal npiece
            g, c = units[u]
            b = npiece % len(MXB)
            npiece += 1
            n = CW if k < c else 128 * (qt + 1)
            bank = ps[:, MXB[b], :]
            lhs = QS[0:ROWS, u % SLOTS, h, 128 * qt:128 * qt + 128]
            rhs = KS[0:ROWS, g % 2, h, CW * k:CW * k + n]
            diag = k == c
            t = put("tensor", lambda e: e.matmul(bank[:, 0:n], lhs, rhs, start=True,
                    stop=not diag), [ap_free[b], qload[u], kload[g], *scr_all],
                    None if diag else s_ap)
            if diag:
                t = put("tensor", lambda e: e.matmul(bank[:, n - 128:n], idb[:, :], mask_q[:, :],
                        start=False, stop=True), [t_mask, t_c], s_ap)
            dst = mp[:, u % 2, 4 * h + qt, k:k + 1]
            ap_free[b] = put("vector", lambda e: e.tensor_reduce(dst, bank[:, 0:n], AX.X, ALU.max),
                             [t], s_mx)

        def row_max(u):
            nonlocal npiece
            g, c = units[u]
            b = npiece % len(MXB)
            npiece += 1
            bank = ps[:, MXB[b], :]
            t = put("vector", lambda e: e.tensor_reduce(mm[:, :], mp[:, u % 2, :, 0:c + 1], AX.X,
                    ALU.max), [(s_mx, s_mx.n), (s_mt, s_mt.n)], s_ms)
            t = put("tensor", lambda e: e.transpose(bank[0:16, 0:128], mm[:, :], idf[:, :]),
                    [t, ap_free[b]], s_mt)
            t = put("vector", lambda e: e.tensor_scalar(m1[:, 0, :], bank[0:16, 0:128], -1.0, None,
                    ALU.mult), [t, mw_done.get(u - 1)], s_ms)
            t = put("vector", lambda e: e.scalar_tensor_tensor(
                out=mr[:, :], in0=bank[0:16, 0:128], scalar=-1.0, in1=m1[:, 0, :], op0=ALU.mult,
                op1=ALU.subtract), [t], s_ms)
            ap_free[b] = t
            t = put("vector", lambda e: e.tensor_copy(m1[:, 1, :], mr[:, :]), [t], s_ms)
            t = put("vector", lambda e: e.tensor_tensor(m1[:, 2, :], mr[:, :], m1[:, 1, :],
                    ALU.subtract), [t], s_ms)
            mw_done[u] = put("sync", Dma(mscr[u].rearrange("i (p q) -> p i q", q=128), m1[:, :, :]),
                             [t], s_mw[u % 2])
            s = u % SLOTS
            mload[u] = put("sync", Dma(QS[ROWS:ROWS + 3, s, :, :].rearrange("i h t -> i (h t)"),
                           mscr[u]), [mw_done[u], st_done.get(u - SLOTS)], s_mr[s])

        nst = 0

        def scores(u, kt, h):
            nonlocal nst
            g, c = units[u]
            off = 128 * max(0, kt - 4 * c)
            b = nst % len(STB)
            pb = nst % PBN
            nst += 1
            bank = ps[:, STB[b], :]
            diag = kt >= 4 * c
            lhs = KS[0:ROWS + 3, g % 2, h, 128 * kt:128 * kt + 128]
            rhs = QS[0:ROWS + 3, u % SLOTS, h, off:CW]
            t = put("tensor", lambda e: e.matmul(bank[:, off:CW], lhs, rhs, start=True,
                    stop=not diag), [st_free[b], mload[u], qload[u], kload[g]],
                    None if diag else s_sT)
            if diag:
                t = put("tensor", lambda e: e.matmul(bank[:, off:off + 128], idb[:, :],
                        mask_k[:, :], start=False, stop=True), [t_mask], s_sT)
            st_done[u] = t
            st_free[b] = put("scalar", lambda e: e.activation(PB[:, pb, off:CW], bank[:, off:CW],
                             ACT.Exp, scale=HD ** -0.5), [t, pb_free[pb]], s_ex)
            return st_free[b], pb

        def values(u, kt, done):
            g, c = units[u]
            off = 128 * max(0, kt - 4 * c)
            o = ps[:, OUB[u % 2], :]
            for h in range(GH):
                ex, pb = done[h]
                t = put("tensor", lambda e, h=h, pb=pb: e.matmul(
                    o[32 * h:32 * h + HD + 1, off:CW], V[:, kt, GH * g + h, :],
                    PB[:, pb, off:CW], start=(kt == 0), stop=(kt == 4 * c + 3),
                    tile_position=(0, 32 * h)), [done[-1][0], o_free[u % 2]],
                    s_pv if h == 3 else None)
            for ex, pb in done:
                pb_free[pb] = t
            return t

        def flush(u, t):
            g, c = units[u]
            ob = OB[:, u % 2, :]
            t = put("scalar", lambda e: e.copy(ob, ps[:, OUB[u % 2], :]),
                    [t, *os_done.get(u - 2, [])], s_oc)
            o_free[u % 2] = t
            for h in range(GH):
                put("sync", Dma(oscr[16 * (GH * g + h):16 * (GH * g + h) + 16,
                                     c * CW:(c + 1) * CW], ob[32 * h:32 * h + 16, :]),
                    [t], s_os[u % 2])
                z = put("sync", Dma(dscr[GH * g + h:GH * g + h + 1, c * CW:(c + 1) * CW],
                                    ob[32 * h + 16:32 * h + 17, :]), [t], s_os[u % 2])
            os_done[u] = [z]

        def row_max_pieces():
            for u, (g, c) in enumerate(units):
                for h in range(GH):
                    for qt in range(4):
                        for k in range(c + 1):
                            piece(u, h, qt, k)
                            if (h, qt, k) == (GH - 1, 3, c):
                                row_max(u)
                            yield

        W1 = wres[:, 0:2048].rearrange("p (k n) -> p k n", k=2)
        W2 = wres[:, 2048:4096].rearrange("p (k n) -> p k n", k=2)
        H1 = wres[:, 4096:12288].rearrange("p (k n) -> p k n", k=8)
        W3 = wres[:, 12288:14336].rearrange("p (k n) -> p k n", k=8)
        H2 = h2r[:, :].rearrange("p (k n) -> p k n", k=8)
        WP = tail[:, 0:512].rearrange("p (k n) -> p k n", k=2)
        S1 = tail[:, 512:520]
        S2 = tail[:, 520:528]
        G1 = tail[:, 528:536]
        G2 = tail[:, 536:544]
        STG = [tail[:, 2048 + 512 * i:2560 + 512 * i] for i in range(2)]
        LO = wst[:, 0:512]
        HI = wst[:, 512:1024]
        h2hi = nc.dram_tensor("h2_hi", (F, F), F32, kind="Internal").ap()
        lows = {n: nc.dram_tensor(f"low_{n}", shape, F32, kind="Internal").ap()
                for n, shape in (("w1", (D, F)), ("w2", (D, F)), ("h1", (F, F)), ("h2", (F, F)),
                                 ("w3", (F, D)))}
        s_wx = [sem("s_wx0"), sem("s_wx1")]
        s_wh = sem("s_wh")
        s_wb = sem("s_wb")
        s_wa = sem("s_wa")
        s_wd = sem("s_wd")
        s_we = sem("s_we")
        s_wl = sem("s_wl")
        free4 = [*scr_all, parts_done[NC - 1], (s_tr, s_tr.n), t_pv[NC - 1]]

        def split_weights():
            n = 0
            abs_done, lo_out, hi_out = {}, None, None
            put("sync", Dma(WP, w_proj.rearrange("(k p) n -> p k n", p=128)), free4, s_wl)
            for dst, src in ((S1, w1_s), (S2, w2_s), (G1, h1_s), (G2, h2_s)):
                put("sync", Dma(dst, src), free4, s_wl)
            for name, src, res in (("w1", w1t, W1), ("w2", w2t, W2), ("h1", h1t, H1),
                                   ("h2", h2t, None), ("w3", w3t, W3)):
                K, N = src.shape
                kk, nn = max(1, 512 // N), min(512, N)
                for k in range(0, K // 128, kk):
                    for j in range(0, N, nn):
                        def part(a):
                            return a.rearrange("(k p) n -> p k n", p=128)[:, k:k + kk, j:j + nn]

                        def flat(a):
                            return a.rearrange("p (k n) -> p k n", k=kk)

                        stage = STG[n % 2]
                        hi = flat(HI) if res is None else res[:, k:k + kk, j:j + nn]
                        t = put("sync", Dma(flat(stage), part(src)),
                                [*free4, abs_done.get(n - 2)], s_wx[n % 2])
                        yield
                        th = put("scalar", lambda e, hi=hi, st=stage: e.copy(hi, flat(st)),
                                 [t, *free4, hi_out if res is None else None], s_wh)
                        yield
                        tl = put("gpsimd", lambda e, hi=hi, st=stage: e.tensor_tensor(
                            flat(LO), flat(st), hi, ALU.subtract), [th, lo_out, (s_wa, s_wa.n)], s_wb)
                        lo_out = put("sync", Dma(part(lows[name]), flat(LO)), [tl], s_wd)
                        if res is None:
                            hi_out = put("sync", Dma(part(h2hi), flat(HI)), [th], s_we)
                        yield
                        abs_done[n] = put("scalar", lambda e, n=n, st=stage: e.activation(
                            st, LO, ACT.Abs, accum_out=acc[:, n:n + 1]), [tl], s_wa)
                        n += 1
                        yield
            self_done.extend([abs_done[n - 1], lo_out, hi_out])

        self_done = []
        split = split_weights()

        length = [4 * c + 4 for _, c in units]
        begin = [sum(length[:u]) for u in range(len(units))]

        def wanted(t):
            return sum(4 * n * min(max((t - (b - n - MARGIN)) / n, 0), 1)
                       for b, n in zip(begin, length))

        for u in range(min(SLOTS, len(units))):
            load_q(u)
        pieces = row_max_pieces()
        queued = step = 0
        late = None
        for u in range(len(units)):
            if u and u + SLOTS - 1 < len(units):
                load_q(u + SLOTS - 1)
            if u % NC == 0 and 2 <= u // NC + 1 < NG:
                for c in range(NC):
                    kload[u // NC + 1] = load_k(u // NC + 1, c, [st_done[u - 1], *scr_all])
            for kt in range(length[u]):
                while queued < wanted(step):
                    next(pieces, None)
                    queued += 1
                goal = wanted(step + 1)
                done = []
                for h in range(GH):
                    done.append(scores(u, kt, h))
                    while queued < goal - (3 - h) * (goal - wanted(step)) / 4:
                        next(pieces, None)
                        queued += 1
                if late is not None:
                    t_last = values(*late)
                    if late[1] == length[late[0]] - 1:
                        flush(late[0], t_last)
                late = (u, kt, done)
                step += 1
                if step > 24 and step % 2:
                    next(split, None)
        for _ in split:
            pass
        t_last = values(*late)
        flush(late[0], t_last)
        u_last = len(units) - 1
        attn = [*os_done[u_last - 1], *os_done[u_last]]
        pe_end = t_last

        XX = [late3[:, 1024 * b:1024 + 1024 * b].rearrange("p (i d) -> p i d", i=4)
              for b in range(2)]
        YY = late3[:, 2048:3072].rearrange("p (i d) -> p i d", i=4)
        OT = late3[:, 3072:4096].rearrange("p (k t) -> p k t", k=2)
        ZZ = late3[:, 3072:4096].rearrange("p (i d) -> p i d", i=4)
        BP = late3[:, 4096:4352]
        S3 = late3[:, 4352:4608]
        DN = tail[:, 1024:2048].rearrange("p (k t) -> p k t", k=2)
        SG = [tail[:, 2048 + 512 * b:2560 + 512 * b] for b in range(2)]
        XT = [[xtr[:, 2048 * b + 1024 * i:2048 * b + 1024 * i + 1024].rearrange(
            "p (k t) -> p k t", k=2) for i in range(2)] for b in range(2)]
        HA = [har[:, 4096 * i:4096 * i + 4096].rearrange("p (k t) -> p k t", k=8) for i in range(2)]
        HB = [hbr[:, 4096 * i:4096 * i + 4096].rearrange("p (k t) -> p k t", k=8) for i in range(2)]
        WL = wlr[:, :]

        for dst, src in ((BP, b_proj), (S3, w3_s)):
            t_wl = put("sync", Dma(dst, src.rearrange("(a n) -> a n", a=1)
                                   .to_broadcast([128, D])), [pe_end], s_wl)
        s_h2 = sem("s_h2")
        t_h2 = put("sync", Dma(H2, h2hi.rearrange("(k p) n -> p k n", p=128)),
                   [pe_end, *self_done], s_h2)
        s_fl = sem("s_fl")
        t = put("vector", lambda e: e.tensor_reduce(accs[:, :], acc[:, :], AX.X, ALU.add),
                self_done, s_fl)
        t = put("tensor", lambda e: e.matmul(ps[0:1, 0, 0:1], accs[:, :], one[:, :], start=True,
                stop=True), [t, (s_ex, s_ex.n), t_c], s_fl)
        t_flag = put("vector", lambda e: e.tensor_copy(flag[:, :], ps[0:1, 0, 0:1]), [t], s_fl)
        P.branch(flag[:, :].bitcast(I32), t_flag)

        s_wr = sem("s_wr")
        s_wf = sem("s_wf")
        low_free = [*self_done]

        def low_weights(name, ks, ns):
            k0, k1 = ks
            n0, n1 = ns
            dst = WL.rearrange("p (k n) -> p k n", k=k1 - k0)[:, :, 0:n1 - n0] \
                if (k1 - k0) * (n1 - n0) == 1024 else \
                WL[:, 0:(k1 - k0) * (n1 - n0)].rearrange("p (k n) -> p k n", k=k1 - k0)
            t = put("sync", Dma(dst, lows[name].rearrange("(k p) n -> p k n", p=128)[
                :, k0:k1, n0:n1]), [t_flag, *low_free], s_wr, general=True)
            return dst, t

        s_in = [sem("s_in0"), sem("s_in1")]
        s_on = sem("s_on")
        s_pj = sem("s_pj")
        s_y = sem("s_y")
        s_x1 = sem("s_res")
        s_t3 = sem("s_t3")
        s_c3 = sem("s_c3")
        s_mm = sem("s_mm")
        s_sg = sem("s_sg")
        s_ha = sem("s_ha")
        s_hb = sem("s_hb")
        s_hc = sem("s_hc")
        s_l4 = sem("s_l4")
        s_z = sem("s_z")
        s_out = [sem("s_o0"), sem("s_o1")]
        last_exp = (s_ex, s_ex.n)
        fin = (s_oc, s_oc.n)
        bank = {b: [last_exp, fin, *ap_free, pe_end] for b in range(8)}
        on_done, pj_done, y_free, t3_done, l1_done, out_done = {}, {}, {}, {}, {}, {}
        ot_free = [pe_end]
        in_done = {}

        def load_in(c):
            for k in range(2):
                put("sync", Dma(OT[:, k, :], oscr[128 * k:128 * k + 128, c * CW:(c + 1) * CW]),
                    [*attn, *os_done[u_last], pe_end, pj_done.get(c - 1), z_done.get(c - 2)],
                    s_in[c % 2])
                for h in range(8):
                    put("sync", Dma(DN[16 * h:16 * h + 16, k, :],
                                    dscr[8 * k + h:8 * k + h + 1, c * CW:(c + 1) * CW]
                                    .to_broadcast([16, CW])), [on_done.get(c - 1)], s_in[c % 2])
            in_done[c] = put("sync", Dma(XX[c % 2], x[c * CW:(c + 1) * CW, :].rearrange(
                "(i p) d -> p i d", p=128)), [out_done.get(c - 2)], s_in[c % 2])

        def front_a(c):
            X, Y = XX[c % 2], YY
            t = put("vector", lambda e: e.reciprocal(DN, DN), [in_done[c]], s_on)
            on_done[c] = t = put("vector", lambda e: e.tensor_tensor(OT, OT, DN, ALU.mult), [t], s_on)
            for i in range(4):
                b = 4 + i % 2
                for k in range(2):
                    tp = put("tensor", lambda e, b=b, i=i, k=k: e.matmul(
                        ps[:, b, 0:D], OT[:, k, 128 * i:128 * i + 128], WP[:, k, :],
                        start=(k == 0), stop=(k == 1)), [t, t_wl, *bank[b]], s_pj if k else None)
                ty = put("vector", lambda e, b=b, i=i: e.tensor_tensor(
                    Y[:, i, :], ps[:, b, 0:D], BP, ALU.add), [tp, t3_done.get(c - 1)], s_y)
                bank[b] = [ty]
            pj_done[c] = tp
            tr = norm_scale([Y[:, i, :] for i in range(4)], [ty])
            for i in range(4):
                t = put("vector", lambda e, i=i: e.tensor_scalar(
                    Y[:, i, :], Y[:, i, :], mv[:, i, 0:1], rstd[:, i:i + 1], ALU.subtract,
                    ALU.mult), [tr], s_y)
            t = put("vector", lambda e: e.tensor_tensor(X, X, Y, ALU.add), [t], s_x1)
            tr = norm_scale([X[:, i, :] for i in range(4)], [t])
            for i in range(4):
                t = put("vector", lambda e, i=i: e.tensor_scalar(
                    Y[:, i, :], X[:, i, :], mv[:, i, 0:1], rstd[:, i:i + 1], ALU.subtract,
                    ALU.mult), [tr], s_y)
            y_free[c] = t

        xt3 = {}

        def front_b(c):
            for k in range(2):
                for i in range(4):
                    t = put("tensor", lambda e, k=k, i=i: e.transpose(
                        ps[:, 6 + k, 128 * i:128 * i + 128], YY[:, i, 128 * k:128 * k + 128],
                        idf[:, :]), [y_free[c], *bank[6 + k]], s_t3)
                th = put("vector", lambda e, k=k: e.tensor_copy(
                    XT[c % 2][0][:, k, :], ps[:, 6 + k, :]), [t, l1_done.get(c - 2)], s_c3)
                tc = put("vector", lambda e, k=k: e.tensor_tensor(
                    XT[c % 2][1][:, k, :], ps[:, 6 + k, :], XT[c % 2][0][:, k, :], ALU.subtract),
                    [th], s_c3)
                bank[6 + k] = [tc]
            t3_done[c] = t
            xt3[c] = tc

        rot = 0
        sg_free = [None, None]
        hb_free, ha_free = None, None

        s_sp = sem("s_sp")

        def product(name, W, m, src, nk, wait):
            nonlocal rot
            b = rot % 4
            rot += 1
            ms = slice(128 * m, 128 * m + 128)
            low, tl = low_weights(name, (0, nk), (128 * m, 128 * m + 128))
            for k in range(nk):
                put("tensor", lambda e, k=k: e.matmul(ps[:, b, :], W[:, k, ms], src[0][:, k, :],
                    start=(k == 0), stop=False), [*wait(k), *bank[b]])
                tw = put("tensor", lambda e, k=k: e.matmul(ps[:, b, :], low[:, k, :],
                         src[0][:, k, :], start=False, stop=False), [tl],
                         s_wf if k == nk - 1 else None, general=True)
                t = put("tensor", lambda e, k=k: e.matmul(ps[:, b, :], W[:, k, ms], src[1][:, k, :],
                        start=False, stop=(k == nk - 1)), (), s_mm if k == nk - 1 else None)
            low_free[:] = [tw]
            return b, t

        def two_parts(a, dst, m, wait):
            th = put("vector", lambda e: e.tensor_copy(dst[0][:, m, :], a), wait, s_sp)
            return put("vector", lambda e: e.tensor_tensor(dst[1][:, m, :], a, dst[0][:, m, :],
                       ALU.subtract), [th], s_sp)

        nsg = 0

        def layer1(c):
            nonlocal nsg
            done = []
            for m in range(8):
                ba_, ta = product("w1", W1, m, XT[c % 2], 2, lambda k: [xt3[c], t_wl])
                bb_, tb = product("w2", W2, m, XT[c % 2], 2, lambda k: [xt3[c], t_wl])
                q = nsg % 2
                nsg += 1
                ts = put("scalar", lambda e, q=q, b=ba_, m=m: e.activation(
                    SG[q], ps[:, b, :], ACT.Silu, scale=S1[:, m:m + 1]), [ta, sg_free[q]], s_sg)
                bank[ba_] = [ts]
                tv = put("vector", lambda e, q=q, b=bb_, m=m: e.scalar_tensor_tensor(
                    out=SG[q], in0=ps[:, b, :], scalar=S2[:, m:m + 1], in1=SG[q],
                    op0=ALU.mult, op1=ALU.mult), [ts, tb, ha_free], s_ha)
                bank[bb_] = [tv]
                sg_free[q] = two_parts(SG[q], HA, m, [tv])
                done.append(sg_free[q])
            l1_done[c] = tb
            return done

        def layer(name, W, S, src, dst, ready, free, s):
            nonlocal nsg
            done = []
            for m in range(8):
                b, t = product(name, W, m, src, 8, lambda k: [ready[k], t_wl, t_h2])
                q = nsg % 2
                nsg += 1
                tg = put("scalar", lambda e, b=b, m=m, q=q: e.activation(
                    SG[q], ps[:, b, :], ACT.Gelu, scale=S[:, m:m + 1]), [t, sg_free[q]], s)
                bank[b] = [tg]
                sg_free[q] = two_parts(SG[q], dst, m, [tg, free])
                done.append(sg_free[q])
            return done, t

        def layer4(c, ready):
            X = XX[c % 2]
            for i in range(4):
                b = 4 + i % 2
                isl = slice(128 * i, 128 * i + 128)
                for k in range(8):
                    if k % 4 == 0:
                        low, tl = low_weights("w3", (k, k + 4), (0, D))
                    put("tensor", lambda e, b=b, isl=isl, k=k: e.matmul(
                        ps[:, b, 0:D], HA[0][:, k, isl], W3[:, k, :], start=(k == 0), stop=False),
                        [ready[k], *bank[b]])
                    tw = put("tensor", lambda e, b=b, isl=isl, k=k, low=low: e.matmul(
                        ps[:, b, 0:D], HA[0][:, k, isl], low[:, k % 4, :], start=False,
                        stop=False), [tl], s_wf if k % 4 == 3 else None, general=True)
                    if k % 4 == 3:
                        low_free[:] = [tw]
                    t = put("tensor", lambda e, b=b, isl=isl, k=k: e.matmul(
                        ps[:, b, 0:D], HA[1][:, k, isl], W3[:, k, :], start=False, stop=(k == 7)),
                        (), s_l4 if k == 7 else None)
                tz = put("vector", lambda e, b=b, i=i: e.tensor_tensor(
                    ZZ[:, i, :], ps[:, b, 0:D], S3, ALU.mult),
                    [t, pj_done.get(c + 1, pj_done[c])], s_z)
                bank[b] = [tz]
            tr = norm_scale([ZZ[:, i, :] for i in range(4)], [tz])
            for i in range(4):
                tz = put("vector", lambda e, i=i: e.tensor_scalar(
                    ZZ[:, i, :], ZZ[:, i, :], mv[:, i, 0:1], rstd[:, i:i + 1], ALU.subtract,
                    ALU.mult), [tr], s_z)
            z_done[c] = tz = put("vector", lambda e: e.tensor_tensor(X, X, ZZ, ALU.add), [tz], s_z)
            out_done[c] = put("sync", Dma(out[c * CW:(c + 1) * CW, :].rearrange(
                "(i p) d -> p i d", p=128), X), [tz], s_out[c % 2])
            return t

        z_done = {}
        load_in(0)
        front_a(0)
        front_b(0)
        if NC > 1:
            load_in(1)
        for c in range(NC):
            r = layer1(c)
            if c + 1 < NC:
                front_a(c + 1)
            r, hap = layer("h1", H1, G1, HA, HB, r, hb_free, s_hb)
            r, hbp = layer("h2", H2, G2, HB, HA, r, hap, s_hc)
            hb_free = hbp
            if c + 1 < NC:
                front_b(c + 1)
            ha_free = layer4(c, r)
            if c + 2 < NC:
                load_in(c + 2)
        put("sync", lambda e: e.nop(), [out_done[NC - 2], out_done[NC - 1]])

        block = ctx.enter_context(nc.Block())

        @block.sync
        def _(e):
            P.run("sync", e)

        @block.tensor
        def _(e):
            P.run("tensor", e)

        @block.vector
        def _(e):
            P.run("vector", e)

        @block.scalar
        def _(e):
            P.run("scalar", e)

        @block.gpsimd
        def _(e):
            P.run("gpsimd", e)


def kernel(**inputs):
    import numpy as np
    import concourse.bacc as bacc
    from concourse import mybir as mb
    from concourse.bass_utils import run_bass_kernel_spmd as run

    def a(name):
        return np.asarray(inputs[name])

    def columns(v):
        return v.reshape(-1, 128).T

    arrays = {
        "x": a("L0_attn_x").reshape(T, D),
        "w_attn": a("L0_attn_w_attn"), "b_attn": a("L0_attn_b_attn"),
        "b_qk": columns(a("L0_attn_b_attn")[0:2 * D]),
        "w_proj": a("L0_attn_w_proj"), "b_proj": a("L0_attn_b_proj"),
        "w1t": a("L0_ffn_w1_w").T, "w1_s": columns(a("L0_ffn_w1_s")),
        "w2t": a("L0_ffn_w2_w").T, "w2_s": columns(a("L0_ffn_w2_s")),
        "h1t": a("L0_ffn_h1_w").T, "h1_s": columns(a("L0_ffn_h1_s")),
        "h2t": a("L0_ffn_h2_w").T, "h2_s": columns(a("L0_ffn_h2_s")),
        "w3t": a("L0_ffn_w3_w").T, "w3_s": a("L0_ffn_w3_s"),
        "ident": np.eye(128, dtype=np.float32),
    }
    arrays = {f"in_{k}": np.ascontiguousarray(v) for k, v in arrays.items()}
    nc = bacc.Bacc("TRN2", target_bir_lowering=False, num_devices=1)
    args = [nc.dram_tensor(k, v.shape, mb.dt.from_np(v.dtype), kind="ExternalInput").ap()
            for k, v in arrays.items()]
    out = nc.dram_tensor("out_0", (T, D), F32, kind="ExternalOutput").ap()
    build(nc, *args, out)
    r = run(nc, [arrays], core_ids=[0])
    return r.results[0]["out_0"].reshape(1, T, D)
```

```python
from contextlib import ExitStack

import concourse.bass as bass
from concourse import mybir

F32 = mybir.dt.float32
BF = mybir.dt.bfloat16
FR = mybir.dt.float32r
I32 = mybir.dt.int32
ALU = mybir.AluOpType
ACT = mybir.ActivationFunctionType
AX = mybir.AxisListType

T = 4096
D = 256
H = 16
HD = 16
F = 1024
CW = 512
NC = T // CW
GH = 4
NG = H // GH
SLOTS = 4
PBN = 8
LSTEP = 3
ORDERS = [[0, 1, 2, 3, 4, 5, 6, 7], [6, 0, 7, 1, 5, 2, 4, 3],
          [3, 4, 2, 5, 1, 7, 0, 6], [7, 6, 5, 4, 3, 2, 1, 0]]
RATE = 1.5
LEAD = 5.0
LEAD_END = 9.0
PIECE = 0.6
STB = [0, 1, 2]
MXB = [3, 4, 5, 6]
OUB = [7]
PAHEAD = 4
MARGIN = 3
NEG = -1.0e30
LOWEST = -3.0e38
ONES = 1.0019378662109375
EPS = 1e-5
KPART = [0, 0, 1, 0, 2, 1]
QPART = [0, 1, 0, 2, 0, 1]
ROWS = 96


class Count:

    def __init__(self, handle):
        self.handle = handle
        self.n = 0


class Program:

    def __init__(self):
        self.queues = {k: [] for k in ("sync", "tensor", "vector", "scalar", "gpsimd")}
        self.turn = None

    def put(self, engine, make, wait=(), inc=None, general=False):
        wait = [w for w in wait if w is not None]
        step = None
        if inc is not None:
            step = 16 if engine == "sync" or isinstance(make, Dma) else 1
            inc.n += step
        self.queues[engine].append((make, wait, inc, step, general))
        return (inc, inc.n) if inc is not None else None

    def branch(self, flag, ready):
        self.turn = {k: len(q) for k, q in self.queues.items()}
        self.flag, self.flag_ready = flag, ready

    def run(self, engine, e):
        queue = self.queues[engine]
        n = self.turn[engine]
        self.emit(e, queue[:n], {})
        if any(q[4] for q in queue[n:]):
            sem, value = self.flag_ready
            e.wait_ge(sem.handle, value)
            flag = e.value_load(self.flag)
            with e.If(flag != 0):
                self.emit(e, queue[n:], {})
            with e.Else():
                self.emit(e, [q for q in queue[n:] if not q[4]], {})
        else:
            self.emit(e, queue[n:], {})

    def emit(self, e, queue, reached):
        for make, wait, inc, step, _ in queue:
            for sem, value in wait:
                if reached.get(id(sem), 0) < value:
                    e.wait_ge(sem.handle, value)
                    reached[id(sem)] = value
            ins = make(e)
            if inc is not None:
                ins.then_inc(inc.handle, step)


class Dma:
    def __init__(self, dst, src):
        self.dst, self.src = (a.bitcast(F32) if a.dtype == FR else a for a in (dst, src))

    def __call__(self, e):
        return e.dma_start(self.dst, self.src)


def build(nc, x, w_attn, b_attn, b_qk, w_proj, b_proj, w1t, w1_s, w2t, w2_s, h1t, h1_s, h2t, h2_s,
          w3t, w3_s, ident, out):
    scr = nc.dram_tensor("qk_parts", (3, 2 * D, T), BF, kind="Internal").ap()
    mscr = nc.dram_tensor("row_max", (NG * NC, 3, GH * CW), BF, kind="Internal").ap()
    oscr = nc.dram_tensor("attn_out", (D, T), F32, kind="Internal").ap()
    dscr = nc.dram_tensor("attn_den", (NC, H, CW), F32, kind="Internal").ap()
    rscr = nc.dram_tensor("attn_rec", (NC, H, CW), F32, kind="Internal").ap()

    ctx = ExitStack()
    with ctx:
        def sb(name, shape, dt=F32):
            return ctx.enter_context(nc.sbuf_tensor(name, shape, dt))

        def sem(name):
            return Count(ctx.enter_context(nc.semaphore(name)))

        base = -(-nc.sbuf_base // 32) * 32
        sb("area", [128, 18432 + 16384 + 8192 + 8704])

        def at(name, first, n, dt=F32):
            return nc.alloc_sbuf_tensor_at(name, [128, n], dt, offset=base + 4 * first)

        A0, A1, A2, A3 = 0, 18432, 18432 + 16384, 18432 + 16384 + 8192
        r4 = at("r4", A0, 18432)
        r1 = at("r1", A1, 16384)
        r2 = at("r2", A2, 8192)
        V = at("V", A3, 8704)[:, :].rearrange("p (t h d) -> p t h d", t=T // 128, h=H)
        wres = at("wres", A0, 14336, FR)
        tail = at("tail", A0 + 14336, 3072)
        wst = at("wst", A0 + 14336 + 3072, 1024, FR)
        h2r = at("h2r", A1, 8192, FR)
        hbr = at("hbr", A1 + 8192, 8192, FR)
        har = at("har", A2, 8192, FR)
        xtr = at("xtr", A3, 4096, FR)
        late3 = at("late3", A3 + 4352, 4352)
        wlr = at("wlr", A0 + 14336 + 3072, 1024, FR)
        acc = sb("acc", [128, 44])
        accs = sb("accs", [128, 1])
        one = sb("one", [128, 1])
        flag = sb("flag", [1, 1])
        idf = sb("idf", [128, 128])
        idb = sb("idb", [128, 128], BF)
        mask_k = sb("mask_k", [128, 128], BF)
        mask_q = sb("mask_q", [128, 512], BF)
        wa = r4[:, 14336:15872].rearrange("p (k n) -> p k n", k=2)
        ba = sb("ba", [128, 4])
        bv = r4[:, 15872:16128]
        stats = sb("stats", [128, 4, 6])
        mv = sb("mv", [128, 4, 2])
        ve = sb("ve", [128, 4])
        rstd = sb("rstd", [128, 4])
        half = sb("half", [128, 4])
        mp = sb("mp", [128, 2, 16, NC])
        mm = sb("mm", [128, 16])
        m1 = sb("m1", [16, 3, 128], BF)
        mr = sb("mr", [16, 128])
        ps = ctx.enter_context(nc.psum_tensor("ps", [128, 8, 512], F32))

        KS = r1[:, :].bitcast(BF).rearrange("p (b h t) -> p b h t", b=2, h=GH)
        QS = r2[:, 0:4096].bitcast(BF).rearrange("p (s h t) -> p s h t", s=SLOTS, h=GH)
        PB = r2[:, 4096:8192].rearrange("p (n t) -> p n t", n=PBN)

        P = Program()
        put = P.put

        s_ld = sem("s_ld")
        s_id = sem("s_id")
        s_c = sem("s_c")
        t_id = put("sync", Dma(idf[:, :], ident), inc=s_id)
        s_w = sem("s_w")
        put("sync", Dma(wa, w_attn.rearrange("(k p) n -> p k n", p=128)), inc=s_w)
        put("sync", Dma(ba[:, :], b_qk), inc=s_w)
        t_w = put("sync", Dma(bv, b_attn[2 * D:3 * D].rearrange("(a n) -> a n", a=1)
                              .to_broadcast([128, D])), inc=s_w)
        put("vector", lambda e: e.memset(half[:, :], -0.5), inc=s_c)
        put("vector", lambda e: e.memset(one[:, :], 1.0), inc=s_c)
        put("vector", lambda e: e.tensor_copy(idb[:, :], idf[:, :]), [t_id], s_c)
        t_c = put("vector", lambda e: e.memset(ps[:, OUB[0]:OUB[-1] + 1, :], 0.0), inc=s_c)
        s_g = sem("s_g")
        t_g = put("gpsimd", lambda e: e.memset(mask_q[:, :], 0.0), inc=s_g)
        t_mask = put("gpsimd", lambda e: e.affine_select(out=mask_q[:, 384:512],
            in_=mask_q[:, 384:512], compare_op=ALU.is_ge, fill=NEG, base=0, pattern=[[-1, 128]],
            channel_multiplier=1), [t_g], s_g)
        t = put("gpsimd", lambda e: e.memset(mask_k[:, :], 0.0), [t_mask], s_g)
        t_mk = put("gpsimd", lambda e: e.affine_select(out=mask_k[:, :], in_=mask_k[:, :],
            compare_op=ALU.is_ge, fill=NEG, base=0, pattern=[[1, 128]], channel_multiplier=-1),
            [t], s_g)
        t = put("gpsimd", lambda e: e.memset(r1[ROWS:ROWS + 3, 0:8192], ONES), [t_mk], s_g)
        t_one = put("gpsimd", lambda e: e.memset(V[:, :, :, HD:HD + 1], 1.0), [t], s_g)
        s_ko = sem("s_ko")

        s_st = sem("s_st")
        s_pw = sem("s_pw")

        def cut(buf):
            v = r4[:, 7168 * buf:7168 * buf + 7168]
            return dict(
                X=v[:, 0:1024].rearrange("p (i d) -> p i d", i=4),
                XT=v[:, 1024:2048].rearrange("p (k t) -> p k t", k=2),
                T0=v[:, 2048:4096].rearrange("p (f t) -> p f t", f=4),
                TP=[v[:, 4096 + 1024 * i:5120 + 1024 * i].bitcast(BF)
                    .rearrange("p (f t) -> p f t", f=4) for i in range(3)])

        bufs = [cut(0), cut(1)]
        s_x = [sem("s_x0"), sem("s_x1")]
        s_xn = sem("s_xn")
        s_tr = sem("s_tr")
        s_xt = sem("s_xt")
        s_qk = sem("s_qk")
        s_t0 = sem("s_t0")
        s_pt = sem("s_pt")
        s_p1 = sem("s_p1")
        s_v = sem("s_v")
        s_ve = sem("s_ve")
        s_ksl = [sem(f"s_k{g}") for g in range(NG)]
        s_ql = [sem(f"s_q{s}") for s in range(SLOTS)]
        parts_done, scr_done, t_pv, v_done, xn_free, xt_done = {}, {}, {}, {}, {}, {}
        scr_sems = [sem("s_scr0"), sem("s_scr1")]
        xload, kload = {}, {}

        ring_free = [t_c] * len(MXB)
        taken = 0

        def take():
            nonlocal taken
            r = taken % len(MXB)
            taken += 1
            return r, ps[:, MXB[r], :]

        def load_x(c):
            b = bufs[c % 2]
            xload[c] = put("sync", Dma(b["X"], x[c * CW:(c + 1) * CW, :].rearrange(
                "(i p) d -> p i d", p=128)), [xn_free.get(c - 2)], s_x[c % 2])

        def load_k(g, c, wait):
            for i in range(6):
                kload[g, c] = put("sync", Dma(
                    KS[16 * i:16 * i + 16, g % 2, :, c * CW:(c + 1) * CW],
                    scr[KPART[i], D + 64 * g:D + 64 * g + 64, c * CW:(c + 1) * CW].rearrange(
                        "(h d) t -> d h t", d=HD)), wait, s_ksl[g])

        def turned_input(c):
            b = bufs[c % 2]
            for i in range(4):
                t = put("vector", lambda e, i=i: e.bn_stats(stats[:, i, :], b["X"][:, i, :]),
                        [xload[c]], s_st)
                yield
            for i in range(4):
                t1 = put("vector", lambda e, i=i: e.bn_aggr(mv[:, i, :], stats[:, i, :]), [t], s_st)
            yield
            t2 = put("vector", lambda e: e.tensor_scalar(ve[:, :], mv[:, :, 0:2].rearrange(
                "p i c -> p c i")[:, 1, :], EPS, None, ALU.add), [t1, t_one2], s_st)
            t_r = put("gpsimd", lambda e: e.tensor_tensor(rstd[:, :], ve[:, :], half[:, :],
                      ALU.pow), [t2], s_pw)
            for _ in range(3):
                yield
            for i in range(4):
                t_xn = put("vector", lambda e, i=i: e.tensor_scalar(
                    b["X"][:, i, :], b["X"][:, i, :], mv[:, i, 0:1], rstd[:, i:i + 1],
                    ALU.subtract, ALU.mult), [t_r], s_xn)
                yield
            for k in range(2):
                r, bank = take()
                for i in range(4):
                    t_tr = put("tensor", lambda e, k=k, i=i, bank=bank: e.transpose(
                        bank[:, 128 * i:128 * i + 128], b["X"][:, i, 128 * k:128 * k + 128],
                        idf[:, :]), [t_xn, ring_free[r], t_id], s_tr)
                xt_done[c] = ring_free[r] = put("scalar", lambda e, k=k, bank=bank: e.copy(
                    b["XT"][:, k, :], bank), [t_tr, t_pv.get(c - 2)], s_xt)
                yield
            xn_free[c] = t_tr
            if c + 2 < NC:
                load_x(c + 2)

        def projections(c):
            b = bufs[c % 2]
            t0, t1, t2, t3 = {}, {}, {}, {}
            for n in range(8):
                if n < 4:
                    r, bank = take()
                    for k in range(2):
                        t = put("tensor", lambda e, f=n, k=k, bank=bank: e.matmul(
                            bank, wa[:, k, 128 * f:128 * f + 128], b["XT"][:, k, :],
                            start=(k == 0), stop=(k == 1)), [xt_done[c], t_w, ring_free[r]],
                            s_qk if k else None)
                    t0[n] = ring_free[r] = put("scalar", lambda e, f=n, bank=bank: e.activation(
                        b["T0"][:, f, :], bank, ACT.Identity, bias=ba[:, f:f + 1]),
                        [t, parts_done.get(c - 2)], s_t0)
                    yield
                if 4 <= n and n % 2 == 0:
                    r, bank = take()
                    for i in (n - 4, n - 3):
                        half_bank = bank[:, 256 * (i % 2):256 * (i % 2) + 256]
                        for k in range(2):
                            t = put("tensor", lambda e, i=i, k=k, o=half_bank: e.matmul(
                                o, b["XT"][:, k, 128 * i:128 * i + 128], wa[:, k, 2 * D:3 * D],
                                start=(k == 0), stop=(k == 1)), [ring_free[r]],
                                s_v if k else None)
                    for i in (n - 4, n - 3):
                        v_done[c] = put("vector", lambda e, i=i, o=bank[
                            :, 256 * (i % 2):256 * (i % 2) + 256]: e.tensor_tensor(
                            V[:, 4 * c + i, :, 0:HD], o.rearrange("p (h d) -> p h d", h=H),
                            bv.rearrange("p (h d) -> p h d", h=H), ALU.add), [t, t_w], s_ve)
                    ring_free[r] = v_done[c]
                    t_pv[c] = t
                    yield
                if 1 <= n < 5:
                    f = n - 1
                    t1[f] = put("scalar", lambda e, f=f: e.copy(
                        b["TP"][0][:, f, :], b["T0"][:, f, :]), [t0[f], scr_done.get(c - 2)], s_p1)
                    yield
                if 2 <= n < 6:
                    f = n - 2
                    t2[f] = put("vector", lambda e, f=f: e.tensor_tensor(
                        b["T0"][:, f, :], b["T0"][:, f, :], b["TP"][0][:, f, :], ALU.subtract),
                        [t1[f]], s_pt)
                    yield
                if 3 <= n < 7:
                    f = n - 3
                    t3[f] = put("vector", lambda e, f=f: e.tensor_copy(
                        b["TP"][1][:, f, :], b["T0"][:, f, :]), [t2[f]], s_pt)
                    yield
                if 4 <= n < 8:
                    f = n - 4
                    parts_done[c] = put("vector", lambda e, f=f: e.tensor_tensor(
                        b["TP"][2][:, f, :], b["T0"][:, f, :], b["TP"][1][:, f, :], ALU.subtract),
                        [t3[f]], s_pt)
                    yield
            for i in range(3):
                scr_done[c] = put("sync", Dma(
                    scr[i].rearrange("(f p) t -> p f t", p=128)[:, :, c * CW:(c + 1) * CW],
                    b["TP"][i]), [parts_done[c]], scr_sems[c % 2])
            load_k(0, c, [scr_done[c]])
            load_q(c)
            load_k(1, c, [scr_done[c]])

        def inputs():
            yield from turned_input(0)
            for c in range(NC):
                ahead = turned_input(c + 1) if c + 1 < NC else iter(())
                for _ in projections(c):
                    yield
                    next(ahead, None)
                for _ in ahead:
                    yield
                yield "chunk"

        load_x(0)
        load_x(1)
        put("gpsimd", lambda e: e.memset(r1[ROWS:ROWS + 3, 8192:16384], ONES), [t_one], s_ko)
        t_one2 = (s_ko, s_ko.n)

        units = []
        for g in range(NG):
            units += [(g, c) for c in ORDERS[g]]
        s_ap = sem("s_ap")
        s_mx = sem("s_mx")
        s_mt = sem("s_mt")
        s_ms = sem("s_ms")
        s_mw = [sem("s_mw0"), sem("s_mw1")]
        s_mr = [sem(f"s_mr{s}") for s in range(SLOTS)]
        s_sT = sem("s_sT")
        s_ex = sem("s_ex")
        s_pv = sem("s_pv")
        s_oc = sem("s_oc")
        s_os = [sem("s_os0"), sem("s_os1")]
        OB = tail[:, 2048:3072].rearrange("p (b t) -> p b t", b=2)
        qload, mload, st_done, os_done, os_of, pv_unit = {}, {}, {}, {}, {}, [None]
        ms_done, mw_done = {}, {}
        st_free = [t_c for b in STB]
        pb_free = [None] * PBN
        o_free = [t_c] * len(OUB)

        def load_q(u):
            g, c = units[u]
            s = u % SLOTS
            for i in range(6):
                qload[u] = put("sync", Dma(
                    QS[16 * i:16 * i + 16, s, :, :],
                    scr[QPART[i], 64 * g:64 * g + 64, c * CW:(c + 1) * CW].rearrange(
                        "(h d) t -> d h t", d=HD)), [scr_done[c], st_done.get(u - SLOTS)], s_ql[s])

        def piece(u, h, qt, k):
            g, c = units[u]
            n = CW if k < c else 128 * (qt + 1)
            b, bank = take()
            lhs = QS[0:ROWS, u % SLOTS, h, 128 * qt:128 * qt + 128]
            rhs = KS[0:ROWS, g % 2, h, CW * k:CW * k + n]
            t = put("tensor", lambda e: e.matmul(bank[:, 0:n], lhs, rhs, start=True,
                    stop=True), [ring_free[b], qload[u], kload[g, k]], s_ap)
            dst = mp[:, u % 2, 4 * h + qt, k:k + 1]
            if k < c:
                ring_free[b] = put("vector", lambda e: e.tensor_reduce(
                    dst, bank[:, 0:n], AX.X, ALU.max), [t], s_mx)
            else:
                ring_free[b] = put("vector", lambda e: e.tensor_tensor_reduce(
                    bank[:, 0:n], bank[:, 0:n], mask_q[:, 512 - n:512], 1.0, LOWEST, ALU.add,
                    ALU.max, dst), [t, t_mask, (s_mx, s_mx.n)], s_mx)

        def row_max(u):
            g, c = units[u]
            b, bank = take()
            t = put("vector", lambda e: e.tensor_reduce(mm[:, :], mp[:, u % 2, :, 0:c + 1], AX.X,
                    ALU.max), [(s_mx, s_mx.n), (s_mt, s_mt.n)], s_ms)
            t = put("tensor", lambda e: e.transpose(bank[0:16, 0:128], mm[:, :], idf[:, :]),
                    [t, ring_free[b]], s_mt)
            t = put("vector", lambda e: e.tensor_scalar(m1[:, 0, :], bank[0:16, 0:128], -1.0, None,
                    ALU.mult), [t, mw_done.get(u - 1)], s_ms)
            t = put("vector", lambda e: e.scalar_tensor_tensor(
                out=mr[:, :], in0=bank[0:16, 0:128], scalar=-1.0, in1=m1[:, 0, :], op0=ALU.mult,
                op1=ALU.subtract), [t], s_ms)
            ring_free[b] = t
            t = put("vector", lambda e: e.tensor_copy(m1[:, 1, :], mr[:, :]), [t], s_ms)
            t = put("vector", lambda e: e.tensor_tensor(m1[:, 2, :], mr[:, :], m1[:, 1, :],
                    ALU.subtract), [t], s_ms)
            mw_done[u] = put("sync", Dma(mscr[u].rearrange("i (p q) -> p i q", q=128), m1[:, :, :]),
                             [t], s_mw[u % 2])
            s = u % SLOTS
            mload[u] = put("sync", Dma(QS[ROWS:ROWS + 3, s, :, :].rearrange("i h t -> i (h t)"),
                           mscr[u]), [mw_done[u], st_done.get(u - SLOTS)], s_mr[s])

        nst = 0

        def scores(u, kt, h):
            nonlocal nst
            g, c = units[u]
            off = 128 * max(0, kt - 4 * c)
            b = nst % len(STB)
            pb = nst % PBN
            nst += 1
            bank = ps[:, STB[b], :]
            lhs = KS[0:ROWS + 3, g % 2, h, 128 * kt:128 * kt + 128]
            rhs = QS[0:ROWS + 3, u % SLOTS, h, off:CW]
            diag = kt >= 4 * c
            t = put("tensor", lambda e: e.matmul(bank[:, off:CW], lhs, rhs, start=True,
                    stop=not diag), [st_free[b], mload[u], qload[u], kload[g, kt // 4], t_one,
                                     t_one2 if g % 2 else None], None if diag else s_sT)
            if diag:
                t = put("tensor", lambda e: e.matmul(bank[:, off:off + 128], idb[:, :],
                        mask_k[:, :], start=False, stop=True), [t_mk], s_sT)
            st_done[u] = t
            st_free[b] = t = put("scalar", lambda e: e.activation(
                PB[:, pb, off:CW], bank[:, off:CW], ACT.Exp, scale=HD ** -0.5),
                [t, pb_free[pb]], s_ex)
            return t, pb

        def values(u, kt, done):
            g, c = units[u]
            off = 128 * max(0, kt - 4 * c)
            o = ps[:, OUB[u % len(OUB)], :]
            for h in range(GH):
                ex, pb = done[h]
                t = put("tensor", lambda e, h=h, pb=pb: e.matmul(
                    o[32 * h:32 * h + HD + 1, off:CW], V[:, kt, GH * g + h, :],
                    PB[:, pb, off:CW], start=(kt == 0), stop=(kt == 4 * c + 3),
                    tile_position=(0, 32 * h)), [done[-1][0], o_free[u % len(OUB)], v_done[kt // 4]],
                    s_pv if h == 3 else None)
            for ex, pb in done:
                pb_free[pb] = t
            return t

        def flush(u, t):
            g, c = units[u]
            ob = OB[:, u % 2, :]
            t = put("scalar", lambda e: e.copy(ob, ps[:, OUB[u % len(OUB)], :]),
                    [t, *os_done.get(u - 2, [])], s_oc)
            o_free[u % len(OUB)] = t
            for h in range(GH):
                put("sync", Dma(oscr[16 * (GH * g + h):16 * (GH * g + h) + 16,
                                     c * CW:(c + 1) * CW], ob[32 * h:32 * h + 16, :]),
                    [t], s_os[u % 2])
                z = put("sync", Dma(dscr[c, GH * g + h:GH * g + h + 1, :],
                                    ob[32 * h + 16:32 * h + 17, :]), [t], s_os[u % 2])
            os_done[u] = [z]
            os_of[c] = [*os_of.get(c, []), z]
            attn.append(z)
            pv_unit[0] = t

        def row_max_pieces():
            for u, (g, c) in enumerate(units):
                for h in range(GH):
                    for qt in range(4):
                        for k in range(c + 1):
                            piece(u, h, qt, k)
                            if (h, qt, k) == (GH - 1, 3, c):
                                row_max(u)
                            yield

        W1 = wres[:, 0:2048].rearrange("p (k n) -> p k n", k=2)
        W2 = wres[:, 2048:4096].rearrange("p (k n) -> p k n", k=2)
        H1 = wres[:, 4096:12288].rearrange("p (k n) -> p k n", k=8)
        W3 = wres[:, 12288:14336].rearrange("p (k n) -> p k n", k=8)
        H2 = h2r[:, :].rearrange("p (k n) -> p k n", k=8)
        WP = tail[:, 0:512].rearrange("p (k n) -> p k n", k=2)
        S1 = tail[:, 512:520]
        S2 = tail[:, 520:528]
        G1 = tail[:, 528:536]
        G2 = tail[:, 536:544]
        S3 = tail[:, 544:800]
        RD = [tail[:, 800 + 64 * i:864 + 64 * i] for i in range(2)]
        STG = [tail[:, 1024 + 512 * i:1536 + 512 * i] for i in range(2)]
        LO = wst[:, 0:512]
        HI = wst[:, 512:1024]
        h2hi = nc.dram_tensor("h2_hi", (F, F), F32, kind="Internal").ap()
        lows = {n: nc.dram_tensor(f"low_{n}", shape, F32, kind="Internal").ap()
                for n, shape in (("w1", (D, F)), ("w2", (D, F)), ("h1", (F, F)), ("h2", (F, F)),
                                 ("w3", (F, D)))}
        s_wx = [sem("s_wx0"), sem("s_wx1")]
        s_wh = sem("s_wh")
        s_wb = sem("s_wb")
        s_wa = sem("s_wa")
        s_wd = sem("s_wd")
        s_we = sem("s_we")
        s_wl = sem("s_wl")

        def split_weights():
            free4 = [scr_done[NC - 2], scr_done[NC - 1], parts_done[NC - 1], (s_tr, s_tr.n),
                     t_pv[NC - 1]]
            n = 0
            abs_done, lo_out, hi_out = {}, None, None
            put("sync", Dma(WP, w_proj.rearrange("(k p) n -> p k n", p=128)), free4, s_wl)
            for dst, src in ((S1, w1_s), (S2, w2_s), (G1, h1_s), (G2, h2_s)):
                put("sync", Dma(dst, src), free4, s_wl)
            put("sync", Dma(S3, w3_s.rearrange("(a n) -> a n", a=1).to_broadcast([128, D])),
                free4, s_wl)
            for name, src, res in (("w1", w1t, W1), ("w2", w2t, W2), ("h1", h1t, H1),
                                   ("h2", h2t, None), ("w3", w3t, W3)):
                K, N = src.shape
                kk, nn = max(1, 512 // N), min(512, N)
                for k in range(0, K // 128, kk):
                    for j in range(0, N, nn):
                        def part(a):
                            return a.rearrange("(k p) n -> p k n", p=128)[:, k:k + kk, j:j + nn]

                        def flat(a):
                            return a.rearrange("p (k n) -> p k n", k=kk)

                        stage = STG[n % 2]
                        hi = flat(HI) if res is None else res[:, k:k + kk, j:j + nn]
                        t = put("sync", Dma(flat(stage), part(src)),
                                [*free4, abs_done.get(n - 2)], s_wx[n % 2])
                        yield
                        th = put("scalar", lambda e, hi=hi, st=stage: e.copy(hi, flat(st)),
                                 [t, *free4, hi_out if res is None else None], s_wh)
                        yield
                        tl = put("gpsimd", lambda e, hi=hi, st=stage: e.tensor_tensor(
                            flat(LO), flat(st), hi, ALU.subtract), [th, lo_out, (s_wa, s_wa.n)], s_wb)
                        lo_out = put("sync", Dma(part(lows[name]), flat(LO)), [tl], s_wd)
                        if res is None:
                            hi_out = put("sync", Dma(part(h2hi), flat(HI)), [th], s_we)
                        yield
                        abs_done[n] = put("scalar", lambda e, n=n, st=stage: e.activation(
                            st, LO, ACT.Abs, accum_out=acc[:, n:n + 1]), [tl], s_wa)
                        n += 1
                        yield
            self_done.extend([abs_done[n - 1], lo_out, hi_out])

        self_done = []
        split = split_weights()

        ORDER = list(range(NC - 1, -1, -1))
        where = {c: n % 2 for n, c in enumerate(ORDER)}
        XX = [late3[:, 1024 * b:1024 + 1024 * b].rearrange("p (i d) -> p i d", i=4)
              for b in range(2)]
        YY = late3[:, 2048:3072].rearrange("p (i d) -> p i d", i=4)
        OT = late3[:, 3072:4096].rearrange("p (k t) -> p k t", k=2)
        ZZ = late3[:, 3072:4096].rearrange("p (i d) -> p i d", i=4)
        BP = late3[:, 4096:4352]
        DN = tail[:, 2048:3072].rearrange("p (k t) -> p k t", k=2)
        DN0 = late3[:, 1024:2048].rearrange("p (k t) -> p k t", k=2)
        SG = [tail[:, 1024 + 512 * b:1536 + 512 * b] for b in range(2)]
        XT = [[xtr[:, 2048 * b + 1024 * i:2048 * b + 1024 * i + 1024].rearrange(
            "p (k t) -> p k t", k=2) for i in range(2)] for b in range(2)]
        HA = [har[:, 4096 * i:4096 * i + 4096].rearrange("p (k t) -> p k t", k=8) for i in range(2)]
        HB = [hbr[:, 4096 * i:4096 * i + 4096].rearrange("p (k t) -> p k t", k=8) for i in range(2)]
        WL = wlr[:, :]
        s_bp = sem("s_bp")
        s_h2 = sem("s_h2")
        s_fl = sem("s_fl")
        s_wr = sem("s_wr")
        s_wf = sem("s_wf")
        s_dn = [sem("s_dn0"), sem("s_dn1")]
        s_rc = sem("s_rc")
        s_rs = [sem("s_rs0"), sem("s_rs1")]
        s_in = [sem("s_in0"), sem("s_in1")]
        s_on = sem("s_on")
        s_pj = sem("s_pj")
        s_y = sem("s_y")
        s_res = sem("s_res")
        s_t3 = sem("s_t3")
        s_c3 = sem("s_c3")
        s_c4 = sem("s_c4")
        s_mm = sem("s_mm")
        s_sg = sem("s_sg")
        s_sp = sem("s_sp")
        s_sq = sem("s_sq")
        s_ha = sem("s_ha")
        s_hb = sem("s_hb")
        s_hc = sem("s_hc")
        s_l4 = sem("s_l4")
        s_z = sem("s_z")
        s_out = [sem("s_o0"), sem("s_o1")]
        on_done, pj_done, t3_done, ha_free, scaled, flag_done = (
            [None], [None], [None], [None], [None], [None])
        rows_done = {}
        s_dr = [sem("s_dr0"), sem("s_dr1")]
        rec_done, in_done, y_ready, xt3, l1_done, out_done, z_ready, z_done = (
            {}, {}, {}, {}, {}, {}, {}, {})
        attn = []

        def load_den(c):
            w = where[c]
            t = put("sync", Dma(RD[w], dscr[c].rearrange("h (j t) -> (h j) t", t=64)),
                    os_of[c], s_dn[w])
            for _ in range(12 if c == ORDER[0] else 5):
                yield
            t = put("vector", lambda e: e.reciprocal(RD[w], RD[w]), [t], s_rc)
            rec_done[c] = put("sync", Dma(rscr[c].rearrange("h (j t) -> (h j) t", t=64), RD[w]),
                              [t], s_rs[w])

        def load_rec(c, dn, free):
            w = where[c]
            for k in range(2):
                for h in range(8):
                    rows_done[c] = put("sync", Dma(dn[16 * h:16 * h + 16, k, :],
                        rscr[c, 8 * k + h:8 * k + h + 1, :].to_broadcast([16, CW])),
                        [rec_done[c], *free], s_dr[w])

        def load_in(c, free):
            w = where[c]
            put("sync", Dma(OT, oscr.rearrange("(k p) t -> p k t", p=128)[
                :, :, c * CW:(c + 1) * CW]), [*os_of[c], *free, pj_done[0], z_done.get(1 - w)],
                s_in[w])
            in_done[c] = put("sync", Dma(XX[w], x[c * CW:(c + 1) * CW, :].rearrange(
                "(i p) d -> p i d", p=128)), [out_done.get(w), on_done[0]], s_in[w])

        def norm_steps(tiles, ready):
            for i, a in enumerate(tiles):
                t = put("vector", lambda e, i=i, a=a: e.bn_stats(stats[:, i, :], a), ready, s_st)
                yield
            for i in range(4):
                t1 = put("vector", lambda e, i=i: e.bn_aggr(mv[:, i, :], stats[:, i, :]), [t], s_st)
            yield
            t2 = put("vector", lambda e: e.tensor_scalar(ve[:, :], mv[:, :, 0:2].rearrange(
                "p i c -> p c i")[:, 1, :], EPS, None, ALU.add), [t1], s_st)
            scaled[0] = put("gpsimd", lambda e: e.tensor_tensor(rstd[:, :], ve[:, :], half[:, :],
                            ALU.pow), [t2], s_pw)
            yield
            yield

        def front_a(c, take, free):
            X, Y = XX[where[c]], YY
            dn = DN0 if c == ORDER[0] else DN
            for k in range(2):
                t = put("vector", lambda e, k=k: e.tensor_tensor(
                    OT[:, k, :], OT[:, k, :], dn[:, k, :], ALU.mult), [in_done[c], rows_done[c]], s_on)
                yield
            on_done[0] = t
            for i in range(4):
                r, bank = take()
                old = free[r] if isinstance(free[r], list) else [free[r]]
                for k in range(2):
                    tp = put("tensor", lambda e, i=i, k=k, bank=bank: e.matmul(
                        bank[:, 0:D], OT[:, k, 128 * i:128 * i + 128], WP[:, k, :],
                        start=(k == 0), stop=(k == 1)), [t, t_wl, *old], s_pj if k else None)
                ty = put("vector", lambda e, i=i, bank=bank: e.tensor_tensor(
                    Y[:, i, :], bank[:, 0:D], BP, ALU.add), [tp, t_bp, t3_done[0]], s_y)
                free[r] = [ty] if isinstance(free[r], list) else ty
                yield
            pj_done[0] = tp
            yield from norm_steps([Y[:, i, :] for i in range(4)], [ty])
            for i in range(4):
                t = put("vector", lambda e, i=i: e.tensor_scalar(
                    Y[:, i, :], Y[:, i, :], mv[:, i, 0:1], rstd[:, i:i + 1], ALU.subtract,
                    ALU.mult), [scaled[0]], s_y)
                yield
            for i in range(4):
                t2 = put("vector", lambda e, i=i: e.tensor_tensor(
                    X[:, i, :], X[:, i, :], Y[:, i, :], ALU.add), [t], s_res)
                yield
            yield from norm_steps([X[:, i, :] for i in range(4)], [t2])
            for i in range(4):
                y_ready[c] = put("vector", lambda e, i=i: e.tensor_scalar(
                    Y[:, i, :], X[:, i, :], mv[:, i, 0:1], rstd[:, i:i + 1], ALU.subtract,
                    ALU.mult), [scaled[0]], s_y)
                yield

        def first_loads():
            nonlocal t_wl, t_bp, t_h2
            for _ in split:
                pass
            t_wl = (s_wl, s_wl.n)
            v_free = [st_done[len(units) - 5], pv_unit[0]]
            t_bp = put("sync", Dma(BP, b_proj.rearrange("(a n) -> a n", a=1)
                                   .to_broadcast([128, D])), v_free, s_bp)
            t_h2 = put("sync", Dma(H2, h2hi.rearrange("(k p) n -> p k n", p=128)),
                       [*v_free, *self_done], s_h2)
            t = put("vector", lambda e: e.tensor_reduce(accs[:, :], acc[:, :], AX.X, ALU.add),
                    self_done, s_fl)
            r, bank = take()
            t = put("tensor", lambda e: e.matmul(bank[0:1, 0:1], accs[:, :], one[:, :], start=True,
                    stop=True), [t, ring_free[r], t_c], s_fl)
            flag_done[0] = ring_free[r] = put("vector", lambda e: e.tensor_copy(
                flag[:, :], bank[0:1, 0:1]), [t], s_fl)

        def first_front(c):
            yield from load_den(c)
            v_free = [st_done[len(units) - 5], pv_unit[0]]
            load_rec(c, DN0, v_free)
            load_in(c, v_free)
            for _ in range(14):
                yield
            yield from front_a(c, take, ring_free)

        t_wl = t_bp = t_h2 = None
        early = iter(())

        length = [4 * c + 4 for _, c in units]
        begin = [sum(length[:u]) for u in range(len(units))]

        clock = [0.0]
        for u, (g, c) in enumerate(units):
            for kt in range(length[u]):
                clock.append(clock[-1] + 0.1 + 1.6 * (1 - max(0, kt - 4 * c) / 4))

        def to_clock(t):
            i = min(max(int(t // 1), 0), len(clock) - 2)
            return clock[i] + (t - i) * (clock[i + 1] - clock[i])

        def to_step(v):
            i = sum(x <= v for x in clock[1:-1])
            return i + (v - clock[i]) / (clock[i + 1] - clock[i])

        due = []
        until = float("inf")
        for u in range(len(units) - 1, NC - 1, -1):
            c = units[u][1]
            until = min(until, to_clock(begin[u]) - (LEAD_END if u >= len(units) - 5 else LEAD))
            low = to_clock(max(begin[NC - 1] - MARGIN, begin[u - 3] + 2))
            n = 4 * GH * (c + 1)
            start = max(until - (PIECE * n + 1.0) / RATE, low)
            due += [start + (until - start) * i / n for i in range(n - 1, -1, -1)]
            until = start
        due = [to_step(v) for v in due[::-1]]
        for i in range(1, len(due)):
            due[i] = max(due[i], due[i - 1])
        for u in range(NC - 1, -1, -1):
            n = length[u]
            due = [begin[u] - n - MARGIN + i / 4 for i in range(4 * n)] + due

        def wanted(t):
            while wanted.n < len(due) and due[wanted.n] < t:
                wanted.n += 1
            return wanted.n

        wanted.n = 0
        pieces = row_max_pieces()
        chunks = inputs()
        ends = [-15, -10] + [2 * c * c - 2 * c - 7 - PAHEAD for c in range(2, NC)]
        per = 60
        chunk = in_chunk = queued = 0

        def advance(upto):
            nonlocal chunk, in_chunk, queued
            t = min(advance.at, upto)
            while True:
                while chunk < NC:
                    first = ends[chunk - 1] if chunk else -40
                    if in_chunk >= per * (t - first) / (ends[chunk] - first) and t < ends[chunk]:
                        break
                    if next(chunks) == "chunk":
                        chunk, in_chunk = chunk + 1, 0
                    else:
                        in_chunk += 1
                while queued < wanted(t):
                    next(pieces)
                    queued += 1
                if t >= upto:
                    break
                t = min(t + 0.1, upto)
            advance.at = t

        advance.at = -40
        step = 0
        late = None
        unloaded = []
        for u in range(len(units)):
            if u and NC <= u + SLOTS - 1 < len(units):
                unloaded.append(u + SLOTS - 1)
            for kt in range(length[u]):
                while unloaded and chunk == NC:
                    load_q(unloaded.pop(0))
                advance(step)
                g = u // NC + 1
                k = step - begin[NC * (g - 1)]
                if 2 <= g < NG and k % 8 == 0 and k < 8 * NC:
                    load_k(g, k // 8, [st_done[NC * (g - 1) - 1]])
                done = []
                for h in range(GH):
                    done.append(scores(u, kt, h))
                    advance(step + (h + 1) / 4)
                if late is not None:
                    t_last = values(*late)
                    if late[1] == length[late[0]] - 1:
                        flush(late[0], t_last)
                late = (u, kt, done)
                step += 1
                if step > 84 and step % 2:
                    next(split, None)
                if u == len(units) - 4 and kt == 0:
                    first_loads()
                    early = first_front(ORDER[0])
                next(early, None)
                if u > len(units) - 4:
                    next(early, None)
        for _ in early:
            pass
        t_last = values(*late)
        flush(late[0], t_last)
        pe_end = t_last
        last_exp = (s_ex, s_ex.n)
        fin = (s_oc, s_oc.n)
        bank_of = list(range(8))
        free8 = [[last_exp, fin, *ring_free, pe_end] for b in range(8)]
        nbank = 0

        def take8():
            nonlocal nbank
            r = nbank % 8
            nbank += 1
            return r, ps[:, r, :]

        P.branch(flag[:, :].bitcast(I32), flag_done[0])
        low_free = [*self_done]

        def low_weights(name, ks, ns):
            k0, k1 = ks
            n0, n1 = ns
            dst = WL[:, 0:(k1 - k0) * (n1 - n0)].rearrange("p (k n) -> p k n", k=k1 - k0)
            t = put("sync", Dma(dst, lows[name].rearrange("(k p) n -> p k n", p=128)[
                :, k0:k1, n0:n1]), [flag_done[0], *low_free], s_wr, general=True)
            return dst, t

        def front_b(c):
            b = XT[where[c]]
            for k in range(2):
                r, bank = take8()
                for i in range(4):
                    t = put("tensor", lambda e, k=k, i=i, bank=bank: e.transpose(
                        bank[:, 128 * i:128 * i + 128], YY[:, i, 128 * k:128 * k + 128],
                        idf[:, :]), [y_ready[c], *free8[r]], s_t3)
                th = put("scalar", lambda e, k=k, bank=bank: e.copy(b[0][:, k, :], bank),
                         [t, l1_done.get(where[c]), pe_end], s_c3)
                t_x = put("vector", lambda e, k=k, bank=bank: e.tensor_tensor(
                    b[1][:, k, :], bank, b[0][:, k, :], ALU.subtract), [th], s_c4)
                free8[r] = [t_x]
                yield
            t3_done[0] = t
            xt3[c] = t_x

        def product(name, W, m, src, nk, wait):
            r, bank = take8()
            ms = slice(128 * m, 128 * m + 128)
            low, tl = low_weights(name, (0, nk), (128 * m, 128 * m + 128))
            for k in range(nk):
                put("tensor", lambda e, k=k: e.matmul(bank, W[:, k, ms], src[0][:, k, :],
                    start=(k == 0), stop=False), [*wait(k), *free8[r]])
                tw = put("tensor", lambda e, k=k: e.matmul(bank, low[:, k, :],
                         src[0][:, k, :], start=False, stop=False), [tl],
                         s_wf if k == nk - 1 else None, general=True)
                t = put("tensor", lambda e, k=k: e.matmul(bank, W[:, k, ms], src[1][:, k, :],
                        start=False, stop=(k == nk - 1)), (), s_mm if k == nk - 1 else None)
            low_free[:] = [tw]
            return r, bank, t

        def two_parts(r, bank, dst, m, wait):
            th = put("scalar", lambda e: e.copy(dst[0][:, m, :], bank), wait, s_sp)
            t = put("vector", lambda e: e.tensor_tensor(dst[1][:, m, :], bank, dst[0][:, m, :],
                    ALU.subtract), [th], s_sq)
            free8[r] = [t]
            return t

        nsg = 0
        sg_free = [None, None]

        def layer1(c, beside):
            nonlocal nsg
            done = []
            src = XT[where[c]]
            last = None
            for m in range(9):
                if m < 8:
                    ra, bank_a, ta = product("w1", W1, m, src, 2, lambda k: [xt3[c], t_wl])
                    rb, bank_b, tb = product("w2", W2, m, src, 2, lambda k: [xt3[c], t_wl])
                    q = nsg % 2
                    nsg += 1
                    ts = put("scalar", lambda e, q=q, m=m, bank=bank_a: e.activation(
                        SG[q], bank, ACT.Silu, scale=S1[:, m:m + 1]), [ta, sg_free[q]], s_sg)
                    free8[ra] = [ts]
                    sg_free[q] = tv = put("vector", lambda e, q=q, m=m, bank=bank_b:
                        e.scalar_tensor_tensor(out=bank, in0=bank, scalar=S2[:, m:m + 1],
                        in1=SG[q], op0=ALU.mult, op1=ALU.mult), [ts, tb], s_ha)
                if last is not None:
                    done.append(two_parts(*last))
                last = (rb, bank_b, HA, m, [tv, pe_end, ha_free[0]])
                for _ in range(LSTEP):
                    next(beside, None)
            l1_done[where[c]] = tb
            return done

        def layer(name, W, S, src, dst, ready, free, s, beside):
            done = []
            for m in range(8):
                r, bank, t = product(name, W, m, src, 8, lambda k: [ready[k], t_wl, t_h2])
                tg = put("scalar", lambda e, m=m, bank=bank: e.activation(
                    bank, bank, ACT.Gelu, scale=S[:, m:m + 1]), [t], s)
                done.append(two_parts(r, bank, dst, m, [tg, pe_end, free]))
                for _ in range(3):
                    next(beside, None)
            return done, t

        def layer4(c, ready):
            for i in range(4):
                r, bank = take8()
                isl = slice(128 * i, 128 * i + 128)
                for k in range(8):
                    if k % 4 == 0:
                        low, tl = low_weights("w3", (k, k + 4), (0, D))
                    put("tensor", lambda e, isl=isl, k=k, bank=bank: e.matmul(
                        bank[:, 0:D], HA[0][:, k, isl], W3[:, k, :], start=(k == 0), stop=False),
                        [ready[k], *free8[r]])
                    tw = put("tensor", lambda e, isl=isl, k=k, low=low, bank=bank: e.matmul(
                        bank[:, 0:D], HA[0][:, k, isl], low[:, k % 4, :], start=False,
                        stop=False), [tl], s_wf if k % 4 == 3 else None, general=True)
                    if k % 4 == 3:
                        low_free[:] = [tw]
                    t = put("tensor", lambda e, isl=isl, k=k, bank=bank: e.matmul(
                        bank[:, 0:D], HA[1][:, k, isl], W3[:, k, :], start=False, stop=(k == 7)),
                        (), s_l4 if k == 7 else None)
                tz = put("vector", lambda e, i=i, bank=bank: e.tensor_tensor(
                    ZZ[:, i, :], bank[:, 0:D], S3, ALU.mult), [t, pj_done[0]], s_z)
                free8[r] = [tz]
            ha_free[0] = t
            z_ready[c] = tz

        def output(c):
            X = XX[where[c]]
            yield from norm_steps([ZZ[:, i, :] for i in range(4)], [z_ready[c]])
            for i in range(4):
                tz = put("vector", lambda e, i=i: e.tensor_scalar(
                    ZZ[:, i, :], ZZ[:, i, :], mv[:, i, 0:1], rstd[:, i:i + 1], ALU.subtract,
                    ALU.mult), [scaled[0]], s_z)
                yield
            z_done[where[c]] = tz = put("vector", lambda e: e.tensor_tensor(X, X, ZZ, ALU.add),
                                        [tz], s_z)
            out_done[where[c]] = put("sync", Dma(out[c * CW:(c + 1) * CW, :].rearrange(
                "(i p) d -> p i d", p=128), X), [tz], s_out[where[c]])
            yield

        def beside_front(c):
            load_in(c, ())
            for _ in range(4):
                yield
            yield from front_a(c, take8, free8)


        for _ in front_b(ORDER[0]):
            pass
        tail_steps = iter(())
        hb_free = None
        def before_front(c, tail):
            den = load_den(c) if c is not None else iter(())
            for _ in den:
                next(tail, None)
                yield
            if c is not None:
                load_rec(c, DN, [*attn, on_done[0]])
            for _ in tail:
                yield

        for n, c in enumerate(ORDER):
            tail_steps = before_front(ORDER[n + 1] if n + 1 < NC else None, tail_steps)
            r = layer1(c, tail_steps)
            for _ in tail_steps:
                pass
            ahead = beside_front(ORDER[n + 1]) if n + 1 < NC else iter(())
            r, hap = layer("h1", H1, G1, HA, HB, r, hb_free, s_hb, ahead)
            r, hb_free = layer("h2", H2, G2, HB, HA, r, hap, s_hc, ahead)
            for _ in ahead:
                pass
            if n + 1 < NC:
                for _ in front_b(ORDER[n + 1]):
                    pass
            layer4(c, r)
            tail_steps = output(c)
        for _ in tail_steps:
            pass
        put("sync", lambda e: e.nop(), [out_done[0], out_done[1]])

        block = ctx.enter_context(nc.Block())

        @block.sync
        def _(e):
            P.run("sync", e)

        @block.tensor
        def _(e):
            P.run("tensor", e)

        @block.vector
        def _(e):
            P.run("vector", e)

        @block.scalar
        def _(e):
            P.run("scalar", e)

        @block.gpsimd
        def _(e):
            P.run("gpsimd", e)


def kernel(**inputs):
    import numpy as np
    import concourse.bacc as bacc
    from concourse import mybir as mb
    from concourse.bass_utils import run_bass_kernel_spmd as run

    def a(name):
        return np.asarray(inputs[name])

    def columns(v):
        return v.reshape(-1, 128).T

    arrays = {
        "x": a("L0_attn_x").reshape(T, D),
        "w_attn": a("L0_attn_w_attn"), "b_attn": a("L0_attn_b_attn"),
        "b_qk": columns(a("L0_attn_b_attn")[0:2 * D]),
        "w_proj": a("L0_attn_w_proj"), "b_proj": a("L0_attn_b_proj"),
        "w1t": a("L0_ffn_w1_w").T, "w1_s": columns(a("L0_ffn_w1_s")),
        "w2t": a("L0_ffn_w2_w").T, "w2_s": columns(a("L0_ffn_w2_s")),
        "h1t": a("L0_ffn_h1_w").T, "h1_s": columns(a("L0_ffn_h1_s")),
        "h2t": a("L0_ffn_h2_w").T, "h2_s": columns(a("L0_ffn_h2_s")),
        "w3t": a("L0_ffn_w3_w").T, "w3_s": a("L0_ffn_w3_s"),
        "ident": np.eye(128, dtype=np.float32),
    }
    arrays = {f"in_{k}": np.ascontiguousarray(v) for k, v in arrays.items()}
    nc = bacc.Bacc("TRN2", target_bir_lowering=False, num_devices=1)
    args = [nc.dram_tensor(k, v.shape, mb.dt.from_np(v.dtype), kind="ExternalInput").ap()
            for k, v in arrays.items()]
    out = nc.dram_tensor("out_0", (T, D), F32, kind="ExternalOutput").ap()
    build(nc, *args, out)
    r = run(nc, [arrays], core_ids=[0])
    return r.results[0]["out_0"].reshape(1, T, D)
```
